# Optimizing a Trainium2 kernel written in Bass

```python
import numpy as np
import jax
import jax.numpy as jnp

def _softmax(x, axis=-1):
    return jax.nn.softmax(x, axis=axis)

def _gelu(x):
    return jax.nn.gelu(x, approximate=True)

def _silu(x):
    return jax.nn.silu(x)

def _sigmoid(x):
    return jax.nn.sigmoid(x)

def _layernorm(x, axis=-1, eps=1e-05):
    m = jnp.mean(x, axis=axis, keepdims=True)
    v = jnp.var(x, axis=axis, keepdims=True)
    return (x - m) / jnp.sqrt(v + eps)

def _scatter_add(tgt, idx, src, axis=0):
    return tgt.at[idx].add(src)

def _segment_sum(src, seg, n):
    return jax.ops.segment_sum(src, seg, n)
kernel_name = 'mk_adaln_d1_jaxref_r4_92e646'

def setup_inputs(seed: int=0):
    np.random.seed(seed)
    _w = jnp.asarray

    def _L0_attn_setup():
        import jax, jax.numpy as jnp
        import numpy as np
        LN_EPS = 1e-05

        def _layernorm(x, w, b):
            mu = jnp.mean(x, axis=-1, keepdims=True)
            var = jnp.mean(jnp.square(x - mu), axis=-1, keepdims=True)
            return (x - mu) * jax.lax.rsqrt(var + LN_EPS) * w + b

        def _s4d(u, log_tau, log_dt, mix, D):
            B, C, T = u.shape
            tau = jax.nn.softplus(log_tau)
            dt = jax.nn.softplus(log_dt)
            t = jnp.arange(T, dtype=jnp.float32)
            E = jnp.exp(-(tau * dt)[:, None] * t[None, :])
            E = jax.lax.stop_gradient(E)
            K = mix @ E
            n = 2 * T
            Uf = jnp.fft.rfft(u, n=n, axis=-1)
            Kf = jnp.fft.rfft(K, n=n, axis=-1)
            y = jnp.fft.irfft(Uf * Kf[None], n=n, axis=-1)[..., :T]
            return y + D[None, :, None] * u
        key = jax.random.key(seed)
        ks = jax.random.split(key, 8)
        B, T, C, N = (4, 1024, 256, 64)
        H = 4 * C
        x = jax.random.normal(ks[0], (B, T, C), dtype=jnp.float32)
        log_tau = jnp.zeros((N,), dtype=jnp.float32)
        log_dt = jnp.zeros((), dtype=jnp.float32)
        mix = jax.random.normal(ks[1], (C, N), dtype=jnp.float32) * 0.02
        D = jnp.ones((C,), dtype=jnp.float32)
        norm1_w = jnp.ones((C,), dtype=jnp.float32)
        norm1_b = jnp.zeros((C,), dtype=jnp.float32)
        norm2_w = jnp.ones((C,), dtype=jnp.float32)
        norm2_b = jnp.zeros((C,), dtype=jnp.float32)
        fc1_w = jax.random.normal(ks[2], (H, C), dtype=jnp.float32) * 0.02
        fc1_b = jnp.zeros((H,), dtype=jnp.float32)
        fc2_w = jax.random.normal(ks[3], (C, H), dtype=jnp.float32) * 0.02
        fc2_b = jnp.zeros((C,), dtype=jnp.float32)
        return {'x': x, 'log_tau': log_tau, 'log_dt': log_dt, 'mix': mix, 'D': D, 'norm1_w': norm1_w, 'norm1_b': norm1_b, 'norm2_w': norm2_w, 'norm2_b': norm2_b, 'fc1_w': fc1_w, 'fc1_b': fc1_b, 'fc2_w': fc2_w, 'fc2_b': fc2_b}
    _L0_attn_in = _L0_attn_setup()

    def _L0_ffn_setup():
        import jax, jax.numpy as jnp
        import numpy as np
        D_MODEL = 256
        key = jax.random.key(seed)
        k_x, k_w, k_a1, k_a2 = jax.random.split(key, 4)
        x = jax.random.normal(k_x, (4, 512, D_MODEL), dtype=jnp.float32)
        weight = jax.random.normal(k_w, (D_MODEL, D_MODEL), dtype=jnp.float32) * 0.02
        aux_weight1 = jax.random.normal(k_a1, (D_MODEL, D_MODEL), dtype=jnp.float32) * 0.02
        aux_weight2 = jax.random.normal(k_a2, (D_MODEL, D_MODEL), dtype=jnp.float32) * 0.02
        bias = jnp.zeros((D_MODEL,), dtype=jnp.float32)
        return {'x': x, 'weight': weight, 'aux_weight1': aux_weight1, 'aux_weight2': aux_weight2, 'bias': bias}
    _L0_ffn_in = _L0_ffn_setup()
    _L0_c = _w((lambda *s: np.random.randn(*s).astype(np.float32) * 0.05)(4, 256))
    _L0_wmod = _w((lambda *s: np.random.randn(*s).astype(np.float32) * 0.05)(256, 6 * 256) * 256 ** (-0.5))
    _d = {'L0_attn_x': _L0_attn_in['x'], 'L0_attn_log_tau': _L0_attn_in['log_tau'], 'L0_attn_log_dt': _L0_attn_in['log_dt'], 'L0_attn_mix': _L0_attn_in['mix'], 'L0_attn_D': _L0_attn_in['D'], 'L0_attn_norm1_w': _L0_attn_in['norm1_w'], 'L0_attn_norm1_b': _L0_attn_in['norm1_b'], 'L0_attn_norm2_w': _L0_attn_in['norm2_w'], 'L0_attn_norm2_b': _L0_attn_in['norm2_b'], 'L0_attn_fc1_w': _L0_attn_in['fc1_w'], 'L0_attn_fc1_b': _L0_attn_in['fc1_b'], 'L0_attn_fc2_w': _L0_attn_in['fc2_w'], 'L0_attn_fc2_b': _L0_attn_in['fc2_b'], 'L0_ffn_weight': _L0_ffn_in['weight'], 'L0_ffn_aux_weight1': _L0_ffn_in['aux_weight1'], 'L0_ffn_aux_weight2': _L0_ffn_in['aux_weight2'], 'L0_ffn_bias': _L0_ffn_in['bias'], 'L0_c': _L0_c, 'L0_wmod': _L0_wmod}
    _x0 = _d['L0_attn_x']
    _d['L0_attn_x'] = jax.random.normal(jax.random.fold_in(jax.random.key(seed), 1), (4, 2048, 256), dtype=_x0.dtype)
    del _x0
    return _d

def reference(L0_attn_x, L0_attn_log_tau, L0_attn_log_dt, L0_attn_mix, L0_attn_D, L0_attn_norm1_w, L0_attn_norm1_b, L0_attn_norm2_w, L0_attn_norm2_b, L0_attn_fc1_w, L0_attn_fc1_b, L0_attn_fc2_w, L0_attn_fc2_b, L0_ffn_weight, L0_ffn_aux_weight1, L0_ffn_aux_weight2, L0_ffn_bias, L0_c, L0_wmod):

    def _L0_attn_ref(x, log_tau, log_dt, mix, D, norm1_w, norm1_b, norm2_w, norm2_b, fc1_w, fc1_b, fc2_w, fc2_b):
        import jax, jax.numpy as jnp
        import numpy as np
        LN_EPS = 1e-05

        def _layernorm(x, w, b):
            mu = jnp.mean(x, axis=-1, keepdims=True)
            var = jnp.mean(jnp.square(x - mu), axis=-1, keepdims=True)
            return (x - mu) * jax.lax.rsqrt(var + LN_EPS) * w + b

        def _s4d(u, log_tau, log_dt, mix, D):
            B, C, T = u.shape
            tau = jax.nn.softplus(log_tau)
            dt = jax.nn.softplus(log_dt)
            t = jnp.arange(T, dtype=jnp.float32)
            E = jnp.exp(-(tau * dt)[:, None] * t[None, :])
            E = jax.lax.stop_gradient(E)
            K = mix @ E
            n = 2 * T
            Uf = jnp.fft.rfft(u, n=n, axis=-1)
            Kf = jnp.fft.rfft(K, n=n, axis=-1)
            y = jnp.fft.irfft(Uf * Kf[None], n=n, axis=-1)[..., :T]
            return y + D[None, :, None] * u
        h = _layernorm(x, norm1_w, norm1_b)
        h2 = _s4d(jnp.swapaxes(h, 1, 2), log_tau, log_dt, mix, D)
        x = x + jnp.swapaxes(h2, 1, 2)
        g = _layernorm(x, norm2_w, norm2_b)
        g = jax.nn.gelu(g @ fc1_w.T + fc1_b, approximate=False)
        g = g @ fc2_w.T + fc2_b
        return x + g

    def _L0_ffn_ref(x, weight, aux_weight1, aux_weight2, bias):
        import jax, jax.numpy as jnp
        import numpy as np
        D_MODEL = 256
        h = jnp.einsum('btc,cd->btd', x, weight)
        h = jnp.einsum('btc,cd->btd', h, aux_weight1)
        h = jnp.einsum('btc,cd->btd', h, aux_weight2)
        return jnp.tanh(h + bias)
    x = L0_attn_x
    mod = (_silu(L0_c) @ L0_wmod).reshape(L0_c.shape[0], 6, 1, -1)
    sa, ca, ga, sb, cb, gb = (mod[:, 0], mod[:, 1], mod[:, 2], mod[:, 3], mod[:, 4], mod[:, 5])
    ga = (2 * (ga >= 0) - 1) * jnp.maximum(jnp.abs(ga), 0.25)
    gb = (2 * (gb >= 0) - 1) * jnp.maximum(jnp.abs(gb), 0.25)
    h = _layernorm(x, axis=-1) * (1 + ca) + sa
    x = x + ga * _L0_attn_ref(h, L0_attn_log_tau, L0_attn_log_dt, L0_attn_mix, L0_attn_D, L0_attn_norm1_w, L0_attn_norm1_b, L0_attn_norm2_w, L0_attn_norm2_b, L0_attn_fc1_w, L0_attn_fc1_b, L0_attn_fc2_w, L0_attn_fc2_b)
    h = _layernorm(x, axis=-1) * (1 + cb) + sb
    x = x + gb * _L0_ffn_ref(h, L0_ffn_weight, L0_ffn_aux_weight1, L0_ffn_aux_weight2, L0_ffn_bias)
    return x

_drawn_inputs = setup_inputs


def setup_inputs(seed=0):
    import zlib

    import numpy as np

    out = dict(_drawn_inputs(seed))
    spreads = {'L0_attn_log_tau': (0.0, 0.8),
     'L0_attn_D': (1.0, 0.2),
     'L0_attn_norm1_w': (1.0, 0.2),
     'L0_attn_norm1_b': (0.0, 0.311),
     'L0_attn_norm2_w': (1.0, 0.6),
     'L0_attn_norm2_b': (0.0, 2.0),
     'L0_attn_fc1_b': (0.0, 0.8),
     'L0_attn_fc2_b': (0.0, 0.345),
     'L0_ffn_bias': (0.0, 1.97)}
    factors = {'L0_ffn_weight': 7.9, 'L0_ffn_aux_weight1': 7.887, 'L0_ffn_aux_weight2': 7.879}
    for name, (base, spread) in spreads.items():
        noise = np.random.default_rng([zlib.crc32(name.encode()), seed]).standard_normal(out[name].shape)
        drawn = base * np.exp(spread * noise) if base else spread * noise
        out[name] = jnp.asarray(drawn.astype(out[name].dtype))
    for name, factor in factors.items():
        out[name] = (out[name] * factor).astype(out[name].dtype)
    return out
```

```python
from contextlib import ExitStack

import concourse.bass as bass
from concourse import mybir

F32 = mybir.dt.float32
F32R = mybir.dt.float32r
ALU = mybir.AluOpType
ACT = mybir.ActivationFunctionType

P = 128
BANK = 512
EPS = 1e-5
GATE_MIN = 0.25
LOG1P_TERMS = 9
FC2_LAG = 3
HID_RING = 4
SLOT_CHANS = 16
SLOTS = 2


def adaln_block(nc, x, log_tau, log_dt, mix, D, n1w, n1b, n2w, n2b, fc1_w, fc1_b, fc2_w, fc2_b,
                w0, w1, w2, fbias, cond, wmod, out):
    B, T, C = x.shape
    N = mix.shape[1]
    HID = fc1_w.shape[0]
    G = T // P
    KB = C // P
    MB = HID // P
    HALF = P // 2
    TILES = G * B
    NMOD = wmod.shape[1] // C
    MOD_BANKS = NMOD * C // BANK
    SA, CA, GA, SB, CB, GB, GAB2 = range(NMOD + 1)
    BANK_CHANS = BANK // TILES
    CONV_BANKS = C // BANK_CHANS
    assert N == HALF and B * C == 2 * BANK and KB == 2 and G % 4 == 0 and 2 * HALF == P

    top = slice(0, HALF)
    bot = slice(HALF, P)

    with ExitStack() as ctx:
        def tile(stack, name, shape, dt=F32, side="left"):
            return stack.enter_context(nc.sbuf_tensor(name, shape, dt, side=side))

        def sem(name):
            return ctx.enter_context(nc.semaphore(name))

        h = tile(ctx, "h", [P, G, B, C])
        p_tab = tile(ctx, "p_tab", [P, G, C])
        ga_t = tile(ctx, "ga_t", [P, B, C])
        gb_t = tile(ctx, "gb_t", [P, B, C])
        gab2_t = tile(ctx, "gab2_t", [P, B, C])
        fb_t = tile(ctx, "fb_t", [P, C])
        ident = tile(ctx, "ident", [P, P])
        n2w_c = tile(ctx, "n2w_c", [P, KB])
        n2b_c = tile(ctx, "n2b_c", [P, KB])
        fc1b_c = tile(ctx, "fc1b_c", [P, MB])
        cb_c = tile(ctx, "cb_c", [P, KB, B])
        sb_c = tile(ctx, "sb_c", [P, KB, B])
        mhalf = tile(ctx, "mhalf", [P, B])
        bn = tile(ctx, "bn", [P, 2, B, 6])
        mv = tile(ctx, "mv", [P, 2, 3, B])
        ve = tile(ctx, "ve", [P, 2, B])
        rstd = tile(ctx, "rstd", [P, 2, 2, B])
        nmr = tile(ctx, "nmr", [P, 2, 2, B])
        wf_hi = tile(ctx, "wf_hi", [P, KB, C], F32R)
        wf_lo = tile(ctx, "wf_lo", [P, KB, C], F32R)

        setup = ExitStack()
        wm = tile(setup, "wm", [P, KB, NMOD * C])
        modr = tile(setup, "modr", [B, NMOD + 1, C])
        gtmp = tile(setup, "gtmp", [B, 2, C])
        b2r = tile(setup, "b2r", [B, C])
        condT = tile(setup, "condT", [P, KB, B])
        sil = tile(setup, "sil", [P, 2, KB, B])
        logs = tile(setup, "logs", [P, 2])
        spl = tile(setup, "spl", [P, 8, 2])
        nega = tile(setup, "nega", [P, 1])
        mixn = tile(setup, "mixn", [P, KB, 2, N])
        mixt = tile(setup, "mixt", [P, C])
        n1w_t = tile(setup, "n1w_t", [P, C])
        n1b_t = tile(setup, "n1b_t", [P, C])
        dcol = tile(setup, "dcol", [P, 2, KB])
        drow = tile(setup, "drow", [P, C])
        mixb = tile(setup, "mixb", [P, C])
        times = tile(setup, "times", [P, 4, P])
        decay = tile(setup, "decay", [P, 3, P])
        ones = tile(setup, "ones", [P, P])
        f_first = tile(setup, "f_first", [HALF, P])
        gk = tile(setup, "gk", [HALF, 2, G + 1])
        f_all = tile(setup, "f_all", [P, G, P])
        kpad = tile(setup, "kpad", [P, KB, P - 1])
        wn = tile(setup, "wn", [P, 3, KB, C])
        wT = tile(setup, "wT", [P, 2, KB, C])
        m12 = tile(setup, "m12", [P, KB, C])
        wf = tile(setup, "wf", [P, KB, C])
        setup.close()
        conv = ExitStack()
        zh = tile(conv, "zh", [P, G, B, C])
        toep = tile(conv, "toep", [P, SLOTS, SLOT_CHANS, HALF])

        early = ExitStack()
        xa = tile(early, "xa", [P, 2, B, C], side="right")
        a_t = tile(early, "a_t", [P, B, C], side="right")
        sa_t = tile(early, "sa_t", [P, B, C], side="right")
        st = tile(early, "st", [P, 2, B, C], side="right")
        ym = tile(early, "ym", [P, B, C], side="right")
        mixw = tile(early, "mixw", [P, C], side="right")
        w_z = tile(early, "w_z", [P, P], side="right")
        e_y = tile(early, "e_y", [P, P], side="right")
        d_g = tile(early, "d_g", [HALF, P], side="right")
        early.close()

        fc1_hi = tile(ctx, "fc1_hi", [P, KB, HID], F32R, side="right")
        fc1_lo = tile(ctx, "fc1_lo", [P, KB, HID], F32R, side="right")
        fc2_hi = tile(ctx, "fc2_hi", [P, MB, C], F32R, side="right")
        fc2_lo = tile(ctx, "fc2_lo", [P, MB, C], F32R, side="right")
        raw = ExitStack()
        w_raw = tile(raw, "w_raw", [P, 2, BANK], side="right")
        raw.close()
        conv.close()

        xr = tile(ctx, "xr", [P, 2, B, C])
        s1 = tile(ctx, "s1", [P, B, C])
        zn = tile(ctx, "zn", [P, B, C])
        zf = tile(ctx, "zf", [P, B, C])
        tb = tile(ctx, "tb", [P, B, C])
        gT = tile(ctx, "gT", [P, KB, BANK])
        g_hi = tile(ctx, "g_hi", [P, KB, BANK], F32R)
        g_lo = tile(ctx, "g_lo", [P, KB, BANK], F32R)
        fT = tile(ctx, "fT", [P, KB, BANK])
        f_hi = tile(ctx, "f_hi", [P, KB, BANK], F32R)
        f_lo = tile(ctx, "f_lo", [P, KB, BANK], F32R)
        gel = tile(ctx, "gel", [P, 2, BANK])
        hid_hi = tile(ctx, "hid_hi", [P, HID_RING, BANK], F32R)
        hid_lo = tile(ctx, "hid_lo", [P, HID_RING, BANK], F32R)

        ps = ctx.enter_context(nc.psum_tensor("ps", [P, 8, BANK], F32))
        acc, f1, tr, fo = (ps[:, 2 * i:2 * i + 2, :] for i in range(4))

        def by_batch(pair):
            return pair.rearrange("p a n -> p (a n)").rearrange("p (b c) -> p b c", c=C)

        mod_d = nc.dram_tensor("mod_d", (B, NMOD + 1, C), F32, kind="Internal").ap()
        toep_d = nc.dram_tensor("toep_d", (HALF, C, HALF), F32, kind="Internal").ap()
        x_g = x.rearrange("b (g p) c -> g p b c", p=P)
        out_g = out.rearrange("b (g p) c -> g p b c", p=P)

        cond_in, logs_in, wmod_in, mix_in, norm1_in = sem("cond_in"), sem("logs_in"), sem("wmod_in"), sem("mix_in"), sem("norm1_in")
        b2_in, ffn_in, columns_in, mod_out, k_out = sem("b2_in"), sem("ffn_in"), sem("columns_in"), sem("mod_out"), sem("k_out")
        a_in, gates_in, mod_columns_in = sem("a_in"), sem("gates_in"), sem("mod_columns_in")
        x_in = [sem("x_in0"), sem("x_in1")]
        toep_in = [sem(f"toep_in{s}") for s in range(SLOTS)]
        fc_in = [sem("fc_in0"), sem("fc_in1")]
        xr_in, stored = [sem("xr_in0"), sem("xr_in1")], sem("stored")
        tables_set, ident_set = sem("tables_set"), sem("ident_set")
        cond_exp, sil_step, log_exp, sp_step = sem("cond_exp"), sem("sil_step"), sem("log_exp"), sem("sp_step")
        mod_mm, mod_step, mod_rows = sem("mod_mm"), sem("mod_step"), sem("mod_rows")
        decay_done, mix_tr, mix_step, wz_tr, wz_done, dg_done = (sem("decay_done"), sem("mix_tr"), sem("mix_step"),
                                                                 sem("wz_tr"), sem("wz_done"), sem("dg_done"))
        k_mm, k_step, k_ready = sem("k_mm"), sem("k_step"), sem("k_ready")
        f_step, f_ready, p_mm, p_done = sem("f_step"), sem("f_ready"), sem("p_mm"), sem("p_done")
        ffn_tr, ffn_trd, ffn_mm, m12_done, wf_done, wf_split = (sem("ffn_tr"), sem("ffn_trd"), sem("ffn_mm"), sem("m12_done"),
                                                                sem("wf_done"), sem("wf_split"))
        bn_done = [sem("bn_x"), sem("bn_h")]
        parts_done = [sem("parts_x"), sem("parts_h")]
        mv_done = [sem("mv_x"), sem("mv_h")]
        ve_done = [sem("ve_x"), sem("ve_h")]
        rstd_done = [sem("rstd_x"), sem("rstd_h")]
        nmr_done = [sem("nmr_x"), sem("nmr_h")]
        z_done, za_done, h_done, zh_done = sem("z_done"), sem("za_done"), sem("h_done"), sem("zh_done")
        z_mm, st_done, y_mul, y_mm, y_added = sem("z_mm"), sem("st_done"), sem("y_mul"), sem("y_mm"), sem("y_added")
        conv_mm, conv_added, p_added = sem("conv_mm"), sem("conv_added"), sem("p_added")
        wt_tr, wt_hi, wt_lo = sem("wt_tr"), sem("wt_hi"), sem("wt_lo")
        zn_done, zn_tr, gT_done, g_split = sem("zn_done"), sem("zn_tr"), sem("gT_done"), sem("g_split")
        fc1_mm, gelu_done, hid_split, fc2_mm = sem("fc1_mm"), sem("gelu_done"), sem("hid_split"), sem("fc2_mm")
        g_hi_done, hid_hi_done, f_hi_done = sem("g_hi_done"), sem("hid_hi_done"), sem("f_hi_done")
        s1_done, s2_done, xg_done, x2_done = sem("s1_done"), sem("s2_done"), sem("xg_done"), sem("x2_done")
        zf_done, zf_tr, fT_done, f_split, f_mm = sem("zf_done"), sem("zf_tr"), sem("fT_done"), sem("f_split"), sem("f_mm")
        fb_done, tanh_done, gated, out_done = sem("fb_done"), sem("tanh_done"), sem("gated"), sem("out_done")

        def live(k):
            return not isinstance(k, int) or 0 <= k < G

        def after(k):
            return not isinstance(k, int) or k >= 0

        def sweep(eng, step, first, last, full_from, full_to):
            for t in range(first, full_from):
                step(t, t % 2)
            with eng.Fori(full_from // 2, (full_to + 1) // 2) as pair:
                for par in range(2):
                    step(pair * 2 + par, par)
            for t in range(full_to + 1, last + 1):
                step(t, t % 2)

        STEPS = dict(first=-1, last=G + 1, full_from=2, full_to=G - 3)

        def group(t, k):
            return t[:, k, :, :] if isinstance(k, int) else t[:, bass.ds(k, 1), :, :].rearrange("p o b c -> p (o b) c")

        def dram_group(t, k):
            return t[k, :, :, :] if isinstance(k, int) else t[bass.ds(k, 1), :, :, :].rearrange("o p b c -> (o p) b c")

        def conv_chans(n):
            return slice(n * BANK_CHANS, (n + 1) * BANK_CHANS)

        def over_batches(t):
            return t.unsqueeze(1).to_broadcast([P, B, C])

        def column(v):
            return v.rearrange("(k p) -> p k", p=P)

        def spread(v, parts):
            return v.unsqueeze(0).to_broadcast([parts, v.shape[0]])

        POOL_TABLES = 14
        N_SP = LOG1P_TERMS + 9
        FC1_BANKS = KB * HID // BANK
        WEIGHT_BANKS = FC1_BANKS + MB * C // BANK
        block = ctx.enter_context(nc.Block())

        def weight_banks(fc1, fc2):
            banks = [fc1[:, k, q * BANK:(q + 1) * BANK] for k in range(KB) for q in range(HID // BANK)]
            return banks + [fc2[:, 2 * q:2 * q + 2, :].rearrange("p m c -> p (m c)") for q in range(MB // 2)]

        @block.sync
        def _(sp):
            def load_x(k, par):
                sp.dma_start(xa[:, par, :, :], dram_group(x_g, k)).then_inc(x_in[par], 16)

            sp.dma_start(wm[:, :, :], wmod.rearrange("(k p) n -> p k n", p=P)).then_inc(wmod_in, 16)
            load_x(0, 0)
            load_x(1, 1)
            sp.dma_start(n1w_t[:, :], spread(n1w, P)).then_inc(norm1_in, 16)
            sp.dma_start(n1b_t[:, :], spread(n1b, P)).then_inc(norm1_in, 16)
            for i, w in enumerate((w0, w1, w2)):
                sp.dma_start(wn[:, i, :, :], w.rearrange("(k p) n -> p k n", p=P)).then_inc(ffn_in, 16)
            sp.dma_start(fb_t[:, :], spread(fbias, P)).then_inc(columns_in, 16)

            sp.wait_ge(mod_rows, 1)
            sp.dma_start(mod_d, modr[:, :, :]).then_inc(mod_out, 16)
            sp.wait_ge(mod_out, 16)

            def rows(q, t, s):
                src = bass.AP(tensor=mod_d.tensor, offset=q * C, ap=[[0, P], [(NMOD + 1) * C, B], [1, C]])
                sp.dma_start(t[:, :, :], src).then_inc(s, 16)

            rows(CA, a_t, a_in)
            rows(SA, sa_t, a_in)
            for q, t in ((GA, ga_t), (GB, gb_t), (GAB2, gab2_t)):
                rows(q, t, gates_in)
            with nc.allow_non_contiguous_dma(reason="a few hundred words, once"):
                for q, t in ((CB, cb_c), (SB, sb_c)):
                    for k in range(KB):
                        src = bass.AP(tensor=mod_d.tensor, offset=q * C + k * P, ap=[[1, P], [(NMOD + 1) * C, B]])
                        sp.dma_start(t[:, k, :], src).then_inc(mod_columns_in, 16)

            sp.wait_ge(k_ready, 1)
            for k in range(KB):
                row = kpad[:, k, :]
                src = bass.AP(tensor=row.tensor, offset=row.offset + HALF - 1, ap=[row.ap[0], [-1, HALF], [1, HALF]])
                sp.dma_start(toep_d[:, k * P:(k + 1) * P, :].rearrange("s c t -> c s t"), src).then_inc(k_out, 16)

            def step_x(k, par):
                sp.wait_ge(h_done, k - 1)
                load_x(k, par)

            def load_toep(slot):
                ring = slot % SLOTS
                for half in range(2):
                    src = toep_d[:, slot * SLOT_CHANS:(slot + 1) * SLOT_CHANS, :]
                    sp.dma_start(toep[half * HALF:(half + 1) * HALF, ring, :, :], src).then_inc(toep_in[ring], 16)

            for k in range(2, 4):
                step_x(k, k % 2)
            sp.wait_ge(k_out, 16 * KB)
            sp.wait_ge(wf_split, 1)
            sp.wait_ge(p_done, G // B)
            for slot in range(SLOTS):
                load_toep(slot)
            with sp.Fori(2, G // 2) as pair:
                for par in range(2):
                    step_x(pair * 2 + par, par)

            sp.wait_ge(y_added, G)
            for q in range(WEIGHT_BANKS):
                if q >= 2:
                    sp.wait_ge(wt_tr, q - 1)
                if q < FC1_BANKS:
                    k, m = q // (MB // 4), q % (MB // 4) * 4
                    src = fc1_w.rearrange("(m p) c -> p m c", p=P)[:, m:m + 4, k * P:(k + 1) * P]
                    dst = w_raw[:, q % 2, :].rearrange("p (m c) -> p m c", m=4)
                else:
                    m = (q - FC1_BANKS) * 2
                    src = fc2_w.rearrange("(k p) n -> p k n", p=P)[:, :, m * P:(m + 2) * P]
                    dst = w_raw[:, q % 2, :].rearrange("p (k n) -> p k n", k=KB)
                sp.dma_start(dst, src).then_inc(fc_in[q % 2], 16)
            for slot in range(SLOTS, C // SLOT_CHANS):
                sp.wait_ge(conv_mm, (slot - SLOTS + 1) * SLOT_CHANS // BANK_CHANS)
                load_toep(slot)

            def step(i, par):
                if live(i - 2):
                    sp.wait_ge(out_done, i - 1)
                    sp.dma_start(dram_group(out_g, i - 2), tb[:, :, :]).then_inc(stored, 16)
                if live(i):
                    if isinstance(i, int) and i == 0:
                        sp.wait_ge(conv_added, CONV_BANKS)
                    sp.dma_start(xr[:, par, :, :], dram_group(x_g, i)).then_inc(xr_in[par], 16)

            sweep(sp, step, **STEPS)
            sp.wait_ge(stored, 16 * G)

        @block.gpsimd
        def _(pool):
            steps = [0]

            def alone(ins):
                steps[0] += 1
                ins.then_inc(tables_set, 1)
                pool.wait_ge(tables_set, steps[0])

            def count(t, pattern, base):
                alone(pool.iota(t, pattern=pattern, base=base, channel_multiplier=0, allow_small_or_imprecise_dtypes=True))

            alone(pool.memset(ones[:, :], 1.0))
            pool.affine_select(out=ident[:, :], in_=ones[:, :], compare_op=ALU.is_equal, fill=0.0, base=0,
                               pattern=[[-1, P]], channel_multiplier=1).then_inc(ident_set, 1)
            pool.wait_ge(ident_set, 1)
            alone(pool.memset(mhalf[:, :], -0.5))
            count(times[:, 0, :], [[1, P]], 0)
            count(times[:, 3, 0:G], [[P, G]], 0)
            count(times[top, 1, :], [[-1, P]], P - 1)
            count(times[bot, 1, 0:HALF], [[-1, HALF]], HALF - 1)
            count(times[top, 2, :], [[1, P]], 1)
            count(times[bot, 2, HALF:P], [[1, HALF]], 1)
            alone(pool.memset(decay[bot, 1, HALF:P], 0.0))
            alone(pool.memset(e_y[bot, 0:HALF], 0.0))
            alone(pool.memset(kpad[:, :, :], 0.0))
            alone(pool.memset(f_all[bot, :, :], 1.0))
            alone(pool.memset(st[top, 0, :, :], 0.0))
            alone(pool.memset(gk[:, :, :], 0.0))
            assert steps[0] == POOL_TABLES

            def rsqrt(which, n, par):
                pool.wait_ge(ve_done[which], n)
                pool.tensor_tensor(rstd[:, which, par, :], ve[:, which, :], mhalf[:, :], ALU.pow) \
                    .then_inc(rstd_done[which], 1)

            def step(t, par):
                k = t + 1
                if live(k):
                    rsqrt(0, k + 1, 1 - par)
                if live(t):
                    rsqrt(1, t + 1, par)
                if live(k):
                    if isinstance(k, int) and k == 0:
                        pool.wait_ge(a_in, 32)
                    pool.wait_ge(z_done, k + 1)
                    pool.tensor_tensor(xa[:, 1 - par, :, :], xa[:, 1 - par, :, :], a_t[:, :, :], ALU.mult).then_inc(za_done, 1)
                    pool.wait_ge(za_done, k + 1)
                    pool.tensor_tensor(group(h, k), xa[:, 1 - par, :, :], sa_t[:, :, :], ALU.add).then_inc(h_done, 1)

            sweep(pool, step, **STEPS)

            pool.wait_ge(p_done, G // B)
            for n in range(CONV_BANKS):
                hc = h[:, :, :, conv_chans(n)]
                pool.wait_ge(conv_added, n + 1)
                pool.tensor_tensor(hc, hc, p_tab[:, :, conv_chans(n)].unsqueeze(2).to_broadcast([P, G, B, BANK_CHANS]),
                                   ALU.add).then_inc(p_added, 1)
            pool.wait_ge(gates_in, 48)

            def main(i, par):
                if live(i - 1):
                    pool.wait_ge(s2_done, i)
                    pool.wait_ge(xg_done, i)
                    pool.tensor_tensor(xr[:, 1 - par, :, :], s1[:, :, :], xr[:, 1 - par, :, :], ALU.add).then_inc(x2_done, 1)
                if live(i - 2):
                    pool.wait_ge(tanh_done, i - 1)
                    pool.tensor_tensor(tb[:, :, :], tb[:, :, :], gb_t[:, :, :], ALU.mult).then_inc(gated, 1)
                if live(i - 1):
                    rsqrt(1, G + i, 1 - par)
                if live(i + 1):
                    rsqrt(0, G + i + 2, 1 - par)
                if live(i):
                    if isinstance(i, int):
                        pool.wait_ge(xr_in[par], (i // 2 + 1) * 16)
                    elif par == 0:
                        pool.wait_ge(xr_in[0], i * 8 + 16)
                    else:
                        pool.wait_ge(xr_in[1], i * 8 + 8)
                    pool.tensor_tensor(xr[:, par, :, :], xr[:, par, :, :], gab2_t[:, :, :], ALU.add).then_inc(xg_done, 1)

            sweep(pool, main, **STEPS)

        @block.scalar
        def _(act):
            with nc.allow_non_contiguous_dma(reason="columns of a few hundred words, once"):
                for k in range(KB):
                    act.dma_start(condT[:, k, :], cond[:, k * P:(k + 1) * P].rearrange("b p -> p b")).then_inc(cond_in, 16)
                act.dma_start(logs[top, 0:1], log_tau.unsqueeze(1)).then_inc(logs_in, 16)
                act.dma_start(logs[bot, 0:1], log_tau.unsqueeze(1)).then_inc(logs_in, 16)
                act.dma_start(logs[:, 1:2], bass.AP(tensor=log_dt.tensor, offset=0, ap=[[0, P], [1, 1]])).then_inc(logs_in, 16)
                for dup in range(2):
                    act.dma_start(mixn[:, :, dup, :], mix.rearrange("(k p) n -> p k n", p=P)).then_inc(mix_in, 16)
                act.dma_start(b2r[:, :], spread(fc2_b, B)).then_inc(b2_in, 16)
                act.dma_start(dcol[:, 0, :], column(D)).then_inc(norm1_in, 16)
                act.dma_start(dcol[:, 1, :], column(n1w)).then_inc(norm1_in, 16)
                act.dma_start(drow[HALF:HALF + 1, :], spread(D, 1)).then_inc(norm1_in, 16)
                act.dma_start(n2w_c[:, :], column(n2w)).then_inc(columns_in, 16)
                act.dma_start(n2b_c[:, :], column(n2b)).then_inc(columns_in, 16)
                act.dma_start(fc1b_c[:, :], column(fc1_b)).then_inc(columns_in, 16)

            act.wait_ge(cond_in, 16 * KB)
            act.activation(sil[:, 0, :, :], condT[:, :, :], ACT.Exp, scale=-1.0).then_inc(cond_exp, 1)
            act.wait_ge(sp_step, 1)
            act.activation(spl[:, 1, :], spl[:, 0, :], ACT.Exp, scale=-1.0).then_inc(log_exp, 1)
            act.wait_ge(sp_step, N_SP)
            act.wait_ge(tables_set, POOL_TABLES)
            act.activation(decay[:, 0, :], times[:, 0, :], ACT.Exp, scale=nega[:, 0:1])
            act.activation(decay[top, 1, :], times[top, 1, :], ACT.Exp, scale=nega[top, 0:1])
            act.activation(decay[bot, 1, 0:HALF], times[bot, 1, 0:HALF], ACT.Exp, scale=nega[bot, 0:1])
            act.activation(decay[:, 2, 0:G], times[:, 3, 0:G], ACT.Exp, scale=nega[:, 0:1])
            act.activation(e_y[top, :], times[top, 2, :], ACT.Exp, scale=nega[top, 0:1])
            act.activation(e_y[bot, HALF:P], times[bot, 2, HALF:P], ACT.Exp, scale=nega[bot, 0:1]).then_inc(decay_done, 1)
            act.wait_ge(ffn_tr, 1)
            act.copy(wT[:, :, :, :].rearrange("p a k c -> p a (k c)"), fo).then_inc(ffn_trd, 1)
            act.wait_ge(ffn_mm, 1)
            act.copy(m12[:, :, :].rearrange("p k c -> p (k c)"), acc[:, 0, :]).then_inc(m12_done, 1)
            act.wait_ge(ffn_mm, 2)
            act.copy(wf[:, :, :].rearrange("p k c -> p (k c)"), acc[:, 1, :]).then_inc(wf_done, 1)
            for r in range(G // B):
                act.wait_ge(p_mm, r + 1)
                act.copy(p_tab[:, r * B:(r + 1) * B, :], by_batch((f1, fo)[r % 2])).then_inc(p_done, 1)

            def normed(out_of, in_of, which, par, done):
                for b in range(B):
                    last = act.activation(out_of[:, b, :], in_of[:, b, :], ACT.Identity,
                                          bias=nmr[:, which, par, b:b + 1], scale=rstd[:, which, par, b:b + 1])
                last.then_inc(done, 1)

            def step(t, par):
                if live(t - 1):
                    act.wait_ge(z_mm, t)
                    if after(t - 3):
                        act.wait_ge(y_mul, t - 2)
                    act.copy(st[bot, 1 - par, :, :], by_batch(acc)[bot, :, :])
                    act.copy(st[top, par, :, :], by_batch(acc)[top, :, :]).then_inc(st_done, 1)
                if live(t + 1):
                    act.wait_ge(nmr_done[0], t + 2)
                    normed(xa[:, 1 - par, :, :], xa[:, 1 - par, :, :], 0, 1 - par, z_done)
                if live(t):
                    if isinstance(t, int) and t == 0:
                        act.wait_ge(wz_done, 1)
                        act.wait_ge(dg_done, 1)
                        act.wait_ge(k_out, 16 * KB)
                        act.wait_ge(mod_out, 16)
                        act.wait_ge(wf_split, 1)
                        act.wait_ge(p_done, G // B)
                    act.wait_ge(nmr_done[1], t + 1)
                    normed(group(zh, t), group(h, t), 1, par, zh_done)

            sweep(act, step, **STEPS)

            act.wait_ge(y_added, G)
            for q, dst in enumerate(weight_banks(fc1_hi, fc2_hi)):
                act.wait_ge(wt_tr, q + 1)
                act.copy(dst, tr[:, q % 2, :]).then_inc(wt_hi, 1)

            act.wait_ge(conv_added, CONV_BANKS)

            def main(i, par):
                def gelu(m):
                    act.wait_ge(fc1_mm, i * MB + m + 1)
                    if m >= 2 or after(i - 1):
                        act.wait_ge(hid_split, i * MB + m - 1)
                    act.activation(gel[:, m % 2, :], f1[:, m % 2, :], ACT.Gelu, bias=fc1b_c[:, m:m + 1]).then_inc(gelu_done, 1)

                def channel_modulated(k):
                    for b in range(B):
                        last = act.activation(fT[:, k, b * P:(b + 1) * P], fo[:, k, b * P:(b + 1) * P], ACT.Identity,
                                              bias=sb_c[:, k, b:b + 1], scale=cb_c[:, k, b:b + 1])
                    last.then_inc(fT_done, 1)

                if live(i):
                    gelu(0)
                if live(i - 2):
                    act.wait_ge(fb_done, i - 1)
                    act.activation(tb[:, :, :], tb[:, :, :], ACT.Tanh).then_inc(tanh_done, 1)
                if live(i):
                    for m in range(1, 4):
                        gelu(m)
                if live(i - 1):
                    act.wait_ge(nmr_done[1], G + i)
                    normed(zf, xr[:, 1 - par, :, :], 1, 1 - par, zf_done)
                if live(i):
                    gelu(4)
                    gelu(5)
                if live(i + 1):
                    act.wait_ge(nmr_done[0], G + i + 2)
                    normed(zn, group(h, i + 1), 0, 1 - par, zn_done)
                if live(i):
                    gelu(6)
                if live(i - 1):
                    act.wait_ge(zf_tr, i)
                    if isinstance(i, int) and i == 1:
                        act.wait_ge(mod_columns_in, 16 * 2 * KB)
                    channel_modulated(0)
                if live(i):
                    gelu(7)
                if live(i - 1):
                    channel_modulated(1)
                if live(i + 1):
                    act.wait_ge(zn_tr, i + 2)
                    if isinstance(i, int) and i == -1:
                        act.wait_ge(columns_in, 64)
                    for k in range(KB):
                        last = act.activation(gT[:, k, :], tr[:, k, :], ACT.Identity,
                                              bias=n2b_c[:, k:k + 1], scale=n2w_c[:, k:k + 1])
                    last.then_inc(gT_done, 1)

            sweep(act, main, **STEPS)

        @block.vector
        def _(v):
            v.wait_ge(cond_exp, 1)
            v.tensor_scalar(sil[:, 0, :, :], sil[:, 0, :, :], 1.0, None, ALU.add).then_inc(sil_step, 1)
            v.wait_ge(sil_step, 1)
            v.reciprocal(sil[:, 1, :, :], sil[:, 0, :, :]).then_inc(sil_step, 1)
            v.wait_ge(sil_step, 2)
            v.tensor_tensor(sil[:, 0, :, :], sil[:, 1, :, :], condT[:, :, :], ALU.mult).then_inc(sil_step, 1)

            done = [0]

            def chain(ins):
                done[0] += 1
                ins.then_inc(sp_step, 1)
                v.wait_ge(sp_step, done[0])

            absx, y, den, s, s2, q, pos = (spl[:, i, :] for i in range(7))
            v.wait_ge(logs_in, 48)
            chain(v.scalar_tensor_tensor(absx, logs[:, :], -1.0, logs[:, :], ALU.mult, ALU.max))
            v.wait_ge(log_exp, 1)
            chain(v.tensor_scalar(den, y, 2.0, None, ALU.add))
            chain(v.reciprocal(s2, den))
            chain(v.tensor_tensor(s, y, s2, ALU.mult))
            chain(v.tensor_tensor(s2, s, s, ALU.mult))
            chain(v.tensor_scalar(q, s2, 1.0 / (2 * LOG1P_TERMS + 1), None, ALU.mult))
            for j in range(LOG1P_TERMS - 1, 0, -1):
                chain(v.scalar_tensor_tensor(q, q, 1.0 / (2 * j + 1), s2, ALU.add, ALU.mult))
            chain(v.scalar_tensor_tensor(q, q, 1.0, s, ALU.add, ALU.mult))
            chain(v.tensor_scalar(pos, logs[:, :], 0.0, None, ALU.max))
            chain(v.scalar_tensor_tensor(q, q, 2.0, pos, ALU.mult, ALU.add))
            chain(v.scalar_tensor_tensor(nega[:, 0:1], q[:, 0:1], -1.0, q[:, 1:2], ALU.mult, ALU.mult))

            v.wait_ge(mod_mm, 1)
            steps = [0]

            def mod(ins):
                steps[0] += 1
                ins.then_inc(mod_step, 1)
                v.wait_ge(mod_step, steps[0])

            rows = [acc[0:B, 0, :], acc[0:B, 1, :], f1[0:B, 0, :]]
            for i, r in enumerate(rows):
                last = v.tensor_copy(modr[:, 2 * i:2 * i + 2, :].rearrange("b a c -> b (a c)"), r)
            mod(last)
            v.tensor_scalar(modr[:, CA, :], modr[:, CA, :], 1.0, None, ALU.add)
            v.tensor_scalar(modr[:, CB, :], modr[:, CB, :], 1.0, None, ALU.add)
            for g in (GA, GB):
                mod(v.tensor_scalar(gtmp[:, 0, :], modr[:, g, :], 0.0, 2.0, ALU.is_ge, ALU.mult))
                mod(v.scalar_tensor_tensor(gtmp[:, 1, :], modr[:, g, :], -1.0, modr[:, g, :], ALU.mult, ALU.max))
                mod(v.tensor_scalar(gtmp[:, 1, :], gtmp[:, 1, :], GATE_MIN, None, ALU.max))
                mod(v.scalar_tensor_tensor(modr[:, g, :], gtmp[:, 0, :], -1.0, gtmp[:, 1, :], ALU.add, ALU.mult))
            v.wait_ge(b2_in, 16)
            v.tensor_tensor(modr[:, GAB2, :], modr[:, GA, :], b2r[:, :], ALU.mult).then_inc(mod_rows, 1)

            v.wait_ge(mix_tr, 1)
            v.wait_ge(norm1_in, 80)
            mixps = f1[:, 1, 0:C]
            v.tensor_tensor(mixw[:, :], mixps, n1w_t[:, :], ALU.mult)
            v.tensor_tensor(mixb[top, :], mixps[top, :], n1b_t[top, :], ALU.mult)
            v.tensor_tensor(mixb[HALF:HALF + 1, :], drow[HALF:HALF + 1, :], n1b_t[HALF:HALF + 1, :], ALU.mult).then_inc(mix_step, 1)
            v.wait_ge(wz_tr, 1)
            v.tensor_copy(w_z[:, :], tr[:, 0, 0:P]).then_inc(wz_done, 1)
            v.wait_ge(decay_done, 1)
            v.wait_ge(ident_set, 1)
            v.tensor_scalar(d_g[:, :], ident[top, :], decay[top, 2, 1:2], None, ALU.mult).then_inc(dg_done, 1)
            v.tensor_tensor(dcol[:, 0, :], dcol[:, 0, :], dcol[:, 1, :], ALU.mult).then_inc(k_step, 1)
            v.wait_ge(k_mm, 1)
            v.tensor_copy(kpad[:, :, HALF - 1:P - 1], tr[:, 1, 0:P].rearrange("p (k d) -> p k d", k=KB)).then_inc(k_step, 1)
            v.wait_ge(k_step, 2)
            v.tensor_tensor(kpad[:, :, HALF - 1], kpad[:, :, HALF - 1], dcol[:, 0, :], ALU.add).then_inc(k_ready, 1)
            v.tensor_tensor_scan(f_first[:, :], ones[top, :], decay[top, 0, :], 0.0, ALU.mult, ALU.add).then_inc(f_step, 1)
            v.wait_ge(f_step, 1)
            v.tensor_scalar(gk[:, 0, 0:G], decay[top, 2, 0:G], f_first[:, P - 1:P], None, ALU.mult).then_inc(f_step, 1)
            v.wait_ge(f_step, 2)
            v.tensor_tensor_scan(gk[:, 1, 1:G + 1], ones[top, 0:G], gk[:, 0, 0:G], 0.0, ALU.mult, ALU.add)
            v.tensor_tensor(f_all[top, :, :], f_first[:, :].unsqueeze(1).to_broadcast([HALF, G, P]),
                            decay[top, 2, 0:G].unsqueeze(2).to_broadcast([HALF, G, P]), ALU.mult).then_inc(f_step, 1)
            v.wait_ge(f_step, 3)
            v.tensor_tensor(f_all[top, :, :], f_all[top, :, :],
                            gk[:, 1, 0:G].unsqueeze(2).to_broadcast([HALF, G, P]), ALU.add).then_inc(f_ready, 1)
            v.wait_ge(wf_done, 1)
            v.tensor_copy(wf_hi[:, :, :], wf[:, :, :]).then_inc(f_step, 1)
            v.wait_ge(f_step, 4)
            v.tensor_tensor(wf_lo[:, :, :], wf[:, :, :], wf_hi[:, :, :].bitcast(F32), ALU.subtract).then_inc(wf_split, 1)

            def statistics(src, which, n):
                for b in range(B):
                    last = v.bn_stats(bn[:, which, b, :], src[:, b, :])
                last.then_inc(bn_done[which], 1)
                _, m0, s0, _, m1, s1_ = (bn[:, which, :, i] for i in range(6))
                both, apart, spread_ = (mv[:, which, i, :] for i in range(3))
                v.wait_ge(bn_done[which], n)
                v.tensor_tensor(both, m0, m1, ALU.add)
                v.tensor_tensor(apart, m0, m1, ALU.subtract)
                v.scalar_tensor_tensor(spread_, s0, C * EPS, s1_, ALU.add, ALU.add).then_inc(parts_done[which], 1)
                v.wait_ge(parts_done[which], n)
                v.scalar_tensor_tensor(apart, apart, 0.25, apart, ALU.mult, ALU.mult).then_inc(mv_done[which], 1)
                v.wait_ge(mv_done[which], n)
                v.scalar_tensor_tensor(ve[:, which, :], spread_, 1.0 / C, apart, ALU.mult, ALU.add) \
                    .then_inc(ve_done[which], 1)

            def shift(which, n, par):
                v.wait_ge(rstd_done[which], n)
                v.scalar_tensor_tensor(nmr[:, which, par, :], mv[:, which, 0, :], -0.5, rstd[:, which, par, :],
                                       ALU.mult, ALU.mult).then_inc(nmr_done[which], 1)

            def step(t, par):
                if live(t + 1):
                    if isinstance(t, int):
                        v.wait_ge(x_in[1 - par], 16 * ((t + 1) // 2 + 1))
                    elif par == 0:
                        v.wait_ge(x_in[1], t * 8 + 16)
                    else:
                        v.wait_ge(x_in[0], t * 8 + 24)
                    statistics(xa[:, 1 - par, :, :], 0, t + 2)
                if live(t):
                    v.wait_ge(h_done, t + 1)
                    statistics(group(h, t), 1, t + 1)
                if live(t + 1):
                    shift(0, t + 2, 1 - par)
                if live(t - 1):
                    v.wait_ge(st_done, t)
                    if after(t - 2):
                        v.wait_ge(y_mm, t - 1)
                    v.tensor_tensor(ym[:, :, :], st[:, 1 - par, :, :], over_batches(mixw[:, :]), ALU.mult).then_inc(y_mul, 1)
                if live(t):
                    shift(1, t + 1, par)
                if live(t - 2):
                    v.wait_ge(y_mm, t - 1)
                    v.tensor_tensor(group(h, t - 2), group(h, t - 2), by_batch(f1), ALU.add).then_inc(y_added, 1)

            sweep(v, step, **STEPS)

            def low_part(lo, whole, hi, done):
                v.tensor_tensor(lo, whole, hi.bitcast(F32), ALU.subtract).then_inc(done, 1)

            for q, (lo, hi) in enumerate(zip(weight_banks(fc1_lo, fc2_lo), weight_banks(fc1_hi, fc2_hi))):
                v.wait_ge(wt_hi, q + 1)
                low_part(lo, tr[:, q % 2, :], hi, wt_lo)

            for n in range(CONV_BANKS):
                v.wait_ge(conv_mm, n + 1)
                hc = h[:, :, :, conv_chans(n)].rearrange("p g b c -> p (g b) c")
                bank = ps[:, n % 4, :].rearrange("p (c t) -> p t c", t=TILES)
                v.tensor_tensor(hc, hc, bank, ALU.add).then_inc(conv_added, 1)

            def main(i, par):
                def split_hidden(m):
                    ring = m % HID_RING
                    v.wait_ge(gelu_done, i * MB + m + 1)
                    if m >= HID_RING or after(i - 1):
                        v.wait_ge(fc2_mm, i * MB + m + 1 - HID_RING)
                    v.tensor_copy(hid_hi[:, ring, :], gel[:, m % 2, :]).then_inc(hid_hi_done, 1)
                    v.wait_ge(hid_hi_done, i * MB + m + 1)
                    low_part(hid_lo[:, ring, :], gel[:, m % 2, :], hid_hi[:, ring, :], hid_split)

                if live(i - 1):
                    v.wait_ge(fc2_mm, i * MB)
                    if after(i - 2):
                        v.wait_ge(x2_done, i - 1)
                    v.tensor_tensor(s1[:, :, :], by_batch(acc), group(h, i - 1), ALU.add).then_inc(s1_done, 1)
                    v.wait_ge(s1_done, i)
                    v.tensor_tensor(s1[:, :, :], s1[:, :, :], ga_t[:, :, :], ALU.mult).then_inc(s2_done, 1)
                if live(i - 2):
                    v.wait_ge(f_mm, i - 1)
                    if after(i - 3):
                        v.wait_ge(stored, 16 * (i - 2))
                    v.tensor_tensor(tb[:, :, :], by_batch(fo), over_batches(fb_t[:, :]), ALU.add).then_inc(fb_done, 1)
                if live(i):
                    split_hidden(0)
                if live(i - 1):
                    v.wait_ge(x2_done, i)
                    statistics(xr[:, 1 - par, :, :], 1, G + i)
                if live(i):
                    split_hidden(1)
                if live(i - 2):
                    v.wait_ge(gated, i - 1)
                    v.tensor_tensor(tb[:, :, :], tb[:, :, :], xr[:, par, :, :], ALU.add).then_inc(out_done, 1)
                if live(i - 1):
                    shift(1, G + i, 1 - par)
                if live(i):
                    split_hidden(2)
                if live(i + 1):
                    statistics(group(h, i + 1), 0, G + i + 2)
                if live(i):
                    split_hidden(3)
                if live(i + 1):
                    shift(0, G + i + 2, 1 - par)
                if live(i):
                    for m in range(4, 8):
                        split_hidden(m)
                if live(i - 1):
                    v.wait_ge(fT_done, KB * i)
                    v.tensor_copy(f_hi[:, :, :], fT[:, :, :]).then_inc(f_hi_done, 1)
                    v.wait_ge(f_hi_done, i)
                    low_part(f_lo[:, :, :], fT[:, :, :], f_hi[:, :, :], f_split)
                if live(i + 1):
                    v.wait_ge(gT_done, i + 2)
                    if after(i):
                        v.wait_ge(fc1_mm, (i + 1) * MB)
                    v.tensor_copy(g_hi[:, :, :], gT[:, :, :]).then_inc(g_hi_done, 1)
                    v.wait_ge(g_hi_done, i + 2)
                    low_part(g_lo[:, :, :], gT[:, :, :], g_hi[:, :, :], g_split)

            v.wait_ge(p_added, CONV_BANKS)
            v.wait_ge(columns_in, 64)
            sweep(v, main, **STEPS)

        @block.tensor
        def _(pe):
            def mm(o, lhs, rhs, start, stop):
                return pe.matmul(o, lhs, rhs, start=start, stop=stop)

            pe.wait_ge(sil_step, 3)
            pe.wait_ge(wmod_in, 16)
            for i, bank in enumerate((acc[0:B, 0, :], acc[0:B, 1, :], f1[0:B, 0, :])):
                for k in range(KB):
                    last = mm(bank, sil[:, 0, k, :], wm[:, k, i * BANK:(i + 1) * BANK], k == 0, k == KB - 1)
            last.then_inc(mod_mm, 1)
            pe.wait_ge(ident_set, 1)
            pe.wait_ge(mix_in, 32)
            for k in range(KB):
                last = pe.transpose(f1[:, 1, k * P:(k + 1) * P], mixn[:, k, :, :].rearrange("p a n -> p (a n)"), ident[:, :])
            last.then_inc(mix_tr, 1)
            pe.wait_ge(decay_done, 1)
            pe.transpose(tr[:, 0, 0:P], decay[:, 1, :], ident[:, :]).then_inc(wz_tr, 1)
            pe.wait_ge(mix_step, 1)
            for k in range(KB):
                last = mm(tr[:, 1, k * HALF:(k + 1) * HALF], mixw[top, k * P:(k + 1) * P], decay[top, 0, 0:HALF], True, True)
            last.then_inc(k_mm, 1)
            pe.wait_ge(ffn_in, 48)
            for i in range(2):
                for kc in range(KB):
                    for kd in range(KB):
                        last = pe.transpose(fo[:, i, kd * C + kc * P:kd * C + (kc + 1) * P],
                                            wn[:, i, kc, kd * P:(kd + 1) * P], ident[:, :])
            last.then_inc(ffn_tr, 1)
            pe.wait_ge(ffn_trd, 1)
            pe.wait_ge(mod_rows, 1)
            for i, rhs in ((1, wn[:, 2, :, :]), (0, m12[:, :, :])):
                if i == 0:
                    pe.wait_ge(m12_done, 1)
                for r in range(KB):
                    for k in range(KB):
                        last = mm(acc[:, 1 - i, r * C:(r + 1) * C], wT[:, i, k, r * P:(r + 1) * P], rhs[:, k, :], k == 0, k == KB - 1)
                last.then_inc(ffn_mm, 1)
            pe.wait_ge(f_ready, 1)
            for r in range(G // B):
                if r >= 2:
                    pe.wait_ge(p_done, r - 1)
                for b in range(B):
                    last = mm(by_batch((f1, fo)[r % 2])[:, b, :], f_all[0:HALF + 1, r * B + b, :], mixb[0:HALF + 1, :], True, True)
                last.then_inc(p_mm, 1)

            def step(t, par):
                if live(t - 1):
                    pe.wait_ge(y_mul, t)
                    if after(t - 2):
                        pe.wait_ge(y_added, t - 1)
                    else:
                        pe.wait_ge(p_done, G // B)
                    for b in range(B):
                        last = mm(by_batch(f1)[:, b, :], e_y[:, :], ym[:, b, :], True, True)
                    last.then_inc(y_mm, 1)
                if live(t):
                    pe.wait_ge(zh_done, t + 1)
                    first = isinstance(t, int) and t == 0
                    if first:
                        pe.wait_ge(wz_done, 1)
                        pe.wait_ge(wf_done, 1)
                        pe.wait_ge(dg_done, 1)
                    else:
                        pe.wait_ge(st_done, t)
                    for b in range(B):
                        last = mm(by_batch(acc)[:, b, :], w_z[:, :], group(zh, t)[:, b, :], True, first)
                        if not first:
                            last = mm(by_batch(acc)[:, b, :], d_g[:, :], st[top, par, b, :], False, True)
                    last.then_inc(z_mm, 1)

            sweep(pe, step, **STEPS)

            for q in range(WEIGHT_BANKS):
                pe.wait_ge(fc_in[q % 2], 16 * (q // 2 + 1))
                if q >= 2:
                    pe.wait_ge(wt_lo, q - 1)
                for j in range(4):
                    to = j if q < FC1_BANKS else j % 2 * 2 + j // 2
                    last = pe.transpose(tr[:, q % 2, to * P:(to + 1) * P], w_raw[:, q % 2, j * P:(j + 1) * P], ident[:, :])
                last.then_inc(wt_tr, 1)

            pe.wait_ge(y_added, G)
            for c in range(C):
                ring, place = c // SLOT_CHANS % SLOTS, c % SLOT_CHANS
                n = c // BANK_CHANS
                if place == 0:
                    pe.wait_ge(toep_in[ring], 32 * (c // SLOT_CHANS // SLOTS + 1))
                if c % BANK_CHANS == 0 and n >= 4:
                    pe.wait_ge(conv_added, n - 3)
                col = c % BANK_CHANS * TILES
                for half in (top, bot):
                    last = mm(ps[half, n % 4, col:col + TILES], toep[half, ring, place, :],
                              zh[half, :, :, c].rearrange("p g b -> p (g b)"), True, True)
                if c % BANK_CHANS == BANK_CHANS - 1:
                    last.then_inc(conv_mm, 1)

            def transposes(dst, src, ready, n, done):
                pe.wait_ge(ready, n)
                for k in range(KB):
                    for b in range(B):
                        last = pe.transpose(dst[:, k, b * P:(b + 1) * P], src[:, b, k * P:(k + 1) * P], ident[:, :])
                last.then_inc(done, 1)

            def main(i, par):
                def fc1(m):
                    if m == 0:
                        pe.wait_ge(g_split, i + 1)
                    if m >= 2 or after(i - 1):
                        pe.wait_ge(gelu_done, i * MB + m - 1)
                    terms = [(w, g, k) for k in range(KB) for w, g in ((fc1_hi, g_hi), (fc1_hi, g_lo), (fc1_lo, g_hi))]
                    for n, (w, g, k) in enumerate(terms):
                        last = mm(f1[:, m % 2, :], w[:, k, m * P:(m + 1) * P], g[:, k, :], n == 0, n == len(terms) - 1)
                    last.then_inc(fc1_mm, 1)

                def fc2(m):
                    ring = m % HID_RING
                    pe.wait_ge(hid_split, i * MB + m + 1)
                    if m == 0 and after(i - 1):
                        pe.wait_ge(s1_done, i)
                    for b in range(B):
                        for n, (w, g) in enumerate(((fc2_hi, hid_hi), (fc2_lo, hid_hi), (fc2_hi, hid_lo))):
                            last = pe.matmul(by_batch(acc)[:, b, :], g[:, ring, b * P:(b + 1) * P], w[:, m, :],
                                             start=m == 0 and n == 0 and b % 2 == 0, stop=m == MB - 1 and n == 2,
                                             skip_group_check=True)
                    last.then_inc(fc2_mm, 1)

                if live(i):
                    for m in range(6):
                        fc1(m)
                        if m >= FC2_LAG:
                            fc2(m - FC2_LAG)
                if live(i - 1):
                    if after(i - 2):
                        pe.wait_ge(fb_done, i - 1)
                    transposes(fo, zf, zf_done, i, zf_tr)
                if live(i):
                    for m in range(6, MB):
                        fc1(m)
                        fc2(m - FC2_LAG)
                if live(i + 1):
                    if after(i):
                        pe.wait_ge(gT_done, i + 1)
                    transposes(tr, zn, zn_done, i + 2, zn_tr)
                if live(i):
                    for m in range(MB - FC2_LAG, MB):
                        fc2(m)
                if live(i - 1):
                    pe.wait_ge(f_split, i)
                    for b in range(B):
                        terms = [(g, w, k) for k in range(KB) for g, w in ((f_hi, wf_hi), (f_hi, wf_lo), (f_lo, wf_hi))]
                        for n, (g, w, k) in enumerate(terms):
                            last = mm(by_batch(fo)[:, b, :], g[:, k, b * P:(b + 1) * P], w[:, k, :], n == 0, n == len(terms) - 1)
                    last.then_inc(f_mm, 1)

            pe.wait_ge(conv_added, CONV_BANKS)
            pe.wait_ge(wt_lo, WEIGHT_BANKS)
            sweep(pe, main, **STEPS)


_INS = ["L0_attn_x", "L0_attn_log_tau", "L0_attn_log_dt", "L0_attn_mix", "L0_attn_D", "L0_attn_norm1_w", "L0_attn_norm1_b",
        "L0_attn_norm2_w", "L0_attn_norm2_b", "L0_attn_fc1_w", "L0_attn_fc1_b", "L0_attn_fc2_w", "L0_attn_fc2_b",
        "L0_ffn_weight", "L0_ffn_aux_weight1", "L0_ffn_aux_weight2", "L0_ffn_bias", "L0_c", "L0_wmod"]


def kernel(**inputs):
    import numpy as _np
    import concourse.bacc as _bacc
    from concourse import mybir as _mybir
    from concourse.bass_utils import run_bass_kernel_spmd as _run

    nc = _bacc.Bacc("TRN2", target_bir_lowering=False, num_devices=1)
    arrays, args = {}, []
    for name in _INS:
        a = _np.ascontiguousarray(inputs[name])
        if a.ndim == 0:
            a = a.reshape(1)
        arrays[f"in_{name}_dram"] = a
        args.append(nc.dram_tensor(f"in_{name}_dram", a.shape, _mybir.dt.from_np(a.dtype), kind="ExternalInput").ap())
    shape = inputs["L0_attn_x"].shape
    args.append(nc.dram_tensor("out_0_dram", shape, _mybir.dt.float32, kind="ExternalOutput").ap())
    adaln_block(nc, *args)
    r = _run(nc, [arrays], core_ids=[0])
    return r.results[0]["out_0_dram"]
```

```python
from contextlib import ExitStack

import concourse.bass as bass
from concourse import mybir

F32 = mybir.dt.float32
F32R = mybir.dt.float32r
ALU = mybir.AluOpType
ACT = mybir.ActivationFunctionType

P = 128
BANK = 512
EPS = 1e-5
GATE_MIN = 0.25
LOG1P_TERMS = 9
FC2_LAG = 3
HID_RING = 4
SLOT_CHANS = 16
SLOTS = 2


def adaln_block(nc, x, log_tau, log_dt, mix, D, n1w, n1b, n2w, n2b, fc1_w, fc1_b, fc2_w, fc2_b,
                w0, w1, w2, fbias, cond, wmod, out):
    B, T, C = x.shape
    N = mix.shape[1]
    HID = fc1_w.shape[0]
    G = T // P
    KB = C // P
    MB = HID // P
    HALF = P // 2
    TILES = G * B
    NMOD = wmod.shape[1] // C
    MOD_BANKS = NMOD * C // BANK
    SA, CA, GA, SB, CB, GB, GAB2 = range(NMOD + 1)
    BANK_CHANS = BANK // TILES
    CONV_BANKS = C // BANK_CHANS
    assert N == HALF and B * C == 2 * BANK and KB == 2 and G % 4 == 0 and 2 * HALF == P

    top = slice(0, HALF)
    bot = slice(HALF, P)

    with ExitStack() as ctx:
        def tile(stack, name, shape, dt=F32, side="left"):
            return stack.enter_context(nc.sbuf_tensor(name, shape, dt, side=side))

        def sem(name):
            return ctx.enter_context(nc.semaphore(name))

        h = tile(ctx, "h", [P, G, B, C])
        p_tab = tile(ctx, "p_tab", [P, G, C])
        ga_t = tile(ctx, "ga_t", [P, B, C])
        gb_t = tile(ctx, "gb_t", [P, B, C])
        gab2_t = tile(ctx, "gab2_t", [P, B, C])
        fb_t = tile(ctx, "fb_t", [P, C])
        ident = tile(ctx, "ident", [P, P])
        n2w_c = tile(ctx, "n2w_c", [P, KB])
        n2b_c = tile(ctx, "n2b_c", [P, KB])
        fc1b_c = tile(ctx, "fc1b_c", [P, MB])
        cb_c = tile(ctx, "cb_c", [P, KB, B])
        sb_c = tile(ctx, "sb_c", [P, KB, B])
        mhalf = tile(ctx, "mhalf", [P, 2, B])
        bn = tile(ctx, "bn", [P, 2, B, 6])
        mv = tile(ctx, "mv", [P, 3, 2, B])
        ve = tile(ctx, "ve", [P, 2, B])
        rstd = tile(ctx, "rstd", [P, 2, 2, B])
        nmr = tile(ctx, "nmr", [P, 2, 2, B])
        wf_hi = tile(ctx, "wf_hi", [P, KB, C], F32R)
        wf_lo = tile(ctx, "wf_lo", [P, KB, C], F32R)

        setup = ExitStack()
        wm = tile(setup, "wm", [P, KB, NMOD * C])
        condT = tile(setup, "condT", [P, KB, B])
        sil = tile(setup, "sil", [P, 2, KB, B])
        logs = tile(setup, "logs", [P, 2])
        spl = tile(setup, "spl", [P, 7, 2])
        nega = tile(setup, "nega", [P, 1])
        mixn = tile(setup, "mixn", [P, KB, 2, N])
        n1w_t = tile(setup, "n1w_t", [P, C])
        n1b_t = tile(setup, "n1b_t", [P, C])
        dcol = tile(setup, "dcol", [P, 2, KB])
        drow = tile(setup, "drow", [P, C])
        times = tile(setup, "times", [P, 4, P])
        decay = tile(setup, "decay", [P, 3, P])
        ones = tile(setup, "ones", [P, P])
        f_first = tile(setup, "f_first", [HALF, P])
        gk = tile(setup, "gk", [HALF, 2, G + 1])
        modr = tile(setup, "modr", [B, NMOD + 1, C])
        gtmp = tile(setup, "gtmp", [B, 2, 2, C])
        b2r = tile(setup, "b2r", [B, C])
        mixb = tile(setup, "mixb", [P, C])
        f_all = tile(setup, "f_all", [P, G, P])
        wn = tile(setup, "wn", [P, 3, KB, C])
        wT = tile(setup, "wT", [P, 2, KB, C])
        m12 = tile(setup, "m12", [P, KB, C])
        wf = tile(setup, "wf", [P, KB, C])
        setup.close()
        conv = ExitStack()
        zh = tile(conv, "zh", [P, G, B, C])
        toep = tile(conv, "toep", [P, SLOTS, SLOT_CHANS, HALF])

        early = ExitStack()
        z = tile(early, "z", [P, 2, B, C], side="right")
        a_t = tile(early, "a_t", [P, B, C], side="right")
        sa_t = tile(early, "sa_t", [P, B, C], side="right")
        st = tile(early, "st", [P, 2, B, C], side="right")
        ym = tile(early, "ym", [P, 2, B, C], side="right")
        mixw = tile(early, "mixw", [P, C], side="right")
        w_z = tile(early, "w_z", [P, P], side="right")
        e_y = tile(early, "e_y", [P, P], side="right")
        d_g = tile(early, "d_g", [HALF, 1], side="right")
        kpad = tile(early, "kpad", [P, KB, P - 1], side="right")
        early.close()

        fc1_hi = tile(ctx, "fc1_hi", [P, KB, HID], F32R, side="right")
        fc1_lo = tile(ctx, "fc1_lo", [P, KB, HID], F32R, side="right")
        fc2_hi = tile(ctx, "fc2_hi", [P, MB, C], F32R, side="right")
        fc2_lo = tile(ctx, "fc2_lo", [P, MB, C], F32R, side="right")
        raw = ExitStack()
        w_raw = tile(raw, "w_raw", [P, 2, BANK], side="right")
        raw.close()
        conv.close()

        xr = tile(ctx, "xr", [P, 2, B, C])
        s1 = tile(ctx, "s1", [P, B, C])
        zn = tile(ctx, "zn", [P, B, C])
        zf = tile(ctx, "zf", [P, B, C])
        tb = tile(ctx, "tb", [P, B, C])
        gT = tile(ctx, "gT", [P, KB, BANK])
        g_hi = tile(ctx, "g_hi", [P, KB, BANK], F32R)
        g_lo = tile(ctx, "g_lo", [P, KB, BANK], F32R)
        fT = tile(ctx, "fT", [P, KB, BANK])
        f_hi = tile(ctx, "f_hi", [P, KB, BANK], F32R)
        f_lo = tile(ctx, "f_lo", [P, KB, BANK], F32R)
        gel = tile(ctx, "gel", [P, 2, BANK])
        hid_hi = tile(ctx, "hid_hi", [P, HID_RING, BANK], F32R)
        hid_lo = tile(ctx, "hid_lo", [P, HID_RING, BANK], F32R)

        ps = ctx.enter_context(nc.psum_tensor("ps", [P, 8, BANK], F32))
        acc, f1, tr, fo = (ps[:, 2 * i:2 * i + 2, :] for i in range(4))

        def by_batch(pair):
            return pair.rearrange("p a n -> p (a n)").rearrange("p (b c) -> p b c", c=C)

        mod_d = nc.dram_tensor("mod_d", (B, NMOD + 1, C), F32, kind="Internal").ap()
        toep_d = nc.dram_tensor("toep_d", (HALF, C, HALF), F32, kind="Internal").ap()
        x_g = x.rearrange("b (g p) c -> g p b c", p=P)
        out_g = out.rearrange("b (g p) c -> g p b c", p=P)

        cond_in, logs_in, wmod_in, mix_in, norm1_in = sem("cond_in"), sem("logs_in"), sem("wmod_in"), sem("mix_in"), sem("norm1_in")
        b2_in, ffn_in, columns_in, mod_out, k_out = sem("b2_in"), sem("ffn_in"), sem("columns_in"), sem("mod_out"), sem("k_out")
        a_in, gates_in, mod_columns_in = sem("a_in"), sem("gates_in"), sem("mod_columns_in")
        x_in = [sem("x_in0"), sem("x_in1")]
        toep_in = [sem(f"toep_in{s}") for s in range(SLOTS)]
        fc_in = [sem("fc_in0"), sem("fc_in1")]
        xr_in, stored = [sem("xr_in0"), sem("xr_in1")], sem("stored")
        tables_set, ident_set = sem("tables_set"), sem("ident_set")
        cond_exp, sil_step, log_exp, sp_step = sem("cond_exp"), sem("sil_step"), sem("log_exp"), sem("sp_step")
        mod_mm, mod_step, mod_copied, mod_a_rows, mod_rows = (sem("mod_mm"), sem("mod_step"), sem("mod_copied"),
                                                              sem("mod_a_rows"), sem("mod_rows"))
        wmod_a_in, mod_a_out = sem("wmod_a_in"), sem("mod_a_out")
        decay_done, mix_tr, mix_step, wz_tr, wz_done, dg_done = (sem("decay_done"), sem("mix_tr"), sem("mix_step"),
                                                                 sem("wz_tr"), sem("wz_done"), sem("dg_done"))
        k_mm, k_step, k_ready = sem("k_mm"), sem("k_step"), sem("k_ready")
        f_step, sums_done, f_ready, p_mm, p_done = sem("f_step"), sem("sums_done"), sem("f_ready"), sem("p_mm"), sem("p_done")
        ffn_tr, ffn_trd, ffn_mm, m12_done, wf_done, wf_split = (sem("ffn_tr"), sem("ffn_trd"), sem("ffn_mm"), sem("m12_done"),
                                                                sem("wf_done"), sem("wf_split"))
        bn_both, parts_both, mv_both, ve_both, rstd_both, nmr_both = (
            sem("bn_both"), sem("parts_both"), sem("mv_both"), sem("ve_both"), sem("rstd_both"), sem("nmr_both"))
        bn_done = [sem("bn_x1"), sem("bn_x2")]
        parts_done = [sem("parts_x1"), sem("parts_x2")]
        mv_done = [sem("mv_x1"), sem("mv_x2")]
        ve_done = [sem("ve_x1"), sem("ve_x2")]
        rstd_done = [sem("rstd_x1"), sem("rstd_x2")]
        nmr_done = [sem("nmr_x1"), sem("nmr_x2")]
        z_done, za_done, h_done, zh_done = sem("z_done"), sem("za_done"), sem("h_done"), sem("zh_done")
        z_mm, st_done, carried, y_mul, y_mm, y_added = sem("z_mm"), sem("st_done"), sem("carried"), sem("y_mul"), sem("y_mm"), sem("y_added")
        conv_mm, conv_added, p_added = sem("conv_mm"), sem("conv_added"), sem("p_added")
        wt_tr, wt_hi, wt_lo = sem("wt_tr"), sem("wt_hi"), sem("wt_lo")
        zn_done, zn_tr, gT_done, g_split = sem("zn_done"), sem("zn_tr"), sem("gT_done"), sem("g_split")
        fc1_mm, gelu_done, hid_split, fc2_mm = sem("fc1_mm"), sem("gelu_done"), sem("hid_split"), sem("fc2_mm")
        g_hi_done, hid_hi_done, f_hi_done = sem("g_hi_done"), sem("hid_hi_done"), sem("f_hi_done")
        s1_done, s2_done, xg_done, x2_done = sem("s1_done"), sem("s2_done"), sem("xg_done"), sem("x2_done")
        zf_done, zf_tr, fT_done, f_split, f_mm = sem("zf_done"), sem("zf_tr"), sem("fT_done"), sem("f_split"), sem("f_mm")
        fb_done, tanh_done, gated, out_done = sem("fb_done"), sem("tanh_done"), sem("gated"), sem("out_done")

        def live(k):
            return not isinstance(k, int) or 0 <= k < G

        def after(k):
            return not isinstance(k, int) or k >= 0

        def sweep(eng, step, first, last, full_from, full_to):
            for t in range(first, full_from):
                step(t, t % 2)
            with eng.Fori(full_from // 2, (full_to + 1) // 2) as pair:
                for par in range(2):
                    step(pair * 2 + par, par)
            for t in range(full_to + 1, last + 1):
                step(t, t % 2)

        def kinds(t):
            return slice(0 if live(t + 2) else 1, 2 if live(t) else 1)

        FIRST_STEPS = dict(first=2, last=G + 2, full_from=4, full_to=G - 3)
        STEPS = dict(first=-1, last=G + 1, full_from=2, full_to=G - 3)

        def group(t, k):
            return t[:, k, :, :] if isinstance(k, int) else t[:, bass.ds(k, 1), :, :].rearrange("p o b c -> p (o b) c")

        def dram_group(t, k):
            return t[k, :, :, :] if isinstance(k, int) else t[bass.ds(k, 1), :, :, :].rearrange("o p b c -> (o p) b c")

        def conv_chans(n):
            return slice(n * BANK_CHANS, (n + 1) * BANK_CHANS)

        CONV_RING = (6, 7, 0, 1, 2, 3)

        def conv_bank(n):
            return ps[:, CONV_RING[n % len(CONV_RING)], :]

        def z_bank(par):
            return by_batch((acc, tr)[par])

        def over_batches(t):
            return t.unsqueeze(1).to_broadcast([P, B, C])

        def column(v):
            return v.rearrange("(k p) -> p k", p=P)

        def spread(v, parts):
            return v.unsqueeze(0).to_broadcast([parts, v.shape[0]])

        POOL_TABLES = 14
        N_SP = LOG1P_TERMS + 9
        FC1_BANKS = KB * HID // BANK
        WEIGHT_BANKS = FC1_BANKS + MB * C // BANK
        assert 2 * WEIGHT_BANKS + 2 <= CONV_BANKS

        def weight_bank_at(n):
            return n // 2 - 1 if n % 2 and 0 < n // 2 <= WEIGHT_BANKS else None

        block = ctx.enter_context(nc.Block())

        def weight_banks(fc1, fc2):
            banks = [fc1[:, k, q * BANK:(q + 1) * BANK] for k in range(KB) for q in range(HID // BANK)]
            return banks + [fc2[:, 2 * q:2 * q + 2, :].rearrange("p m c -> p (m c)") for q in range(MB // 2)]

        @block.sync
        def _(sp):
            def load_x(k, par):
                if not isinstance(k, int):
                    sp.wait_ge(x_in[par], (k - par) * 8)
                elif k >= 2:
                    sp.wait_ge(x_in[par], k // 2 * 16)
                sp.dma_start(group(h, k), dram_group(x_g, k)).then_inc(x_in[par], 16)

            with nc.allow_non_contiguous_dma(reason="columns of a few hundred words, once"):
                w = wmod.rearrange("(k p) n -> p k n", p=P)
                sp.dma_start(wm[:, :, 0:BANK], w[:, :, 0:BANK]).then_inc(wmod_a_in, 16)
                for dup in range(2):
                    sp.dma_start(mixn[:, :, dup, :], mix.rearrange("(k p) n -> p k n", p=P)).then_inc(mix_in, 16)
                sp.dma_start(wm[:, :, BANK:NMOD * C], w[:, :, BANK:NMOD * C]).then_inc(wmod_in, 16)
                load_x(0, 0)
                load_x(1, 1)
                sp.dma_start(n1w_t[:, :], spread(n1w, P)).then_inc(norm1_in, 16)
                sp.dma_start(n1b_t[:, :], spread(n1b, P)).then_inc(norm1_in, 16)
                sp.dma_start(dcol[:, 0, :], column(D)).then_inc(norm1_in, 16)
                sp.dma_start(dcol[:, 1, :], column(n1w)).then_inc(norm1_in, 16)
                sp.dma_start(drow[HALF:HALF + 1, :], spread(D, 1)).then_inc(norm1_in, 16)

            for i, w in enumerate((w0, w1, w2)):
                sp.dma_start(wn[:, i, :, :], w.rearrange("(k p) n -> p k n", p=P)).then_inc(ffn_in, 16)
            load_x(2, 0)
            load_x(3, 1)

            def columns():
                sp.dma_start(b2r[:, :], spread(fc2_b, B)).then_inc(b2_in, 16)
                sp.dma_start(fb_t[:, :], spread(fbias, P)).then_inc(columns_in, 16)
                with nc.allow_non_contiguous_dma(reason="columns of a few hundred words, once"):
                    sp.dma_start(n2w_c[:, :], column(n2w)).then_inc(columns_in, 16)
                    sp.dma_start(n2b_c[:, :], column(n2b)).then_inc(columns_in, 16)
                    sp.dma_start(fc1b_c[:, :], column(fc1_b)).then_inc(columns_in, 16)

            def rows(q, t, s):
                src = bass.AP(tensor=mod_d.tensor, offset=q * C, ap=[[0, P], [(NMOD + 1) * C, B], [1, C]])
                sp.dma_start(t[:, :, :], src).then_inc(s, 16)

            sp.wait_ge(mod_a_rows, 1)
            sp.dma_start(mod_d[:, 0:GA, :], modr[:, 0:GA, :]).then_inc(mod_a_out, 16)
            sp.wait_ge(mod_a_out, 16)
            rows(CA, a_t, a_in)
            rows(SA, sa_t, a_in)
            columns()
            for k in range(4, 6):
                load_x(k, k % 2)
            sp.wait_ge(mod_rows, 1)
            sp.dma_start(mod_d[:, GA:NMOD + 1, :], modr[:, GA:NMOD + 1, :]).then_inc(mod_out, 16)
            sp.wait_ge(mod_out, 16)
            for q, t in ((GA, ga_t), (GB, gb_t), (GAB2, gab2_t)):
                rows(q, t, gates_in)
            with nc.allow_non_contiguous_dma(reason="a few hundred words, once"):
                for q, t in ((CB, cb_c), (SB, sb_c)):
                    for k in range(KB):
                        src = bass.AP(tensor=mod_d.tensor, offset=q * C + k * P, ap=[[1, P], [(NMOD + 1) * C, B]])
                        sp.dma_start(t[:, k, :], src).then_inc(mod_columns_in, 16)

            def store_toep(k):
                row = kpad[:, k, :]
                src = bass.AP(tensor=row.tensor, offset=row.offset + HALF - 1, ap=[row.ap[0], [-1, HALF], [1, HALF]])
                sp.dma_start(toep_d[:, k * P:(k + 1) * P, :].rearrange("s c t -> c s t"), src).then_inc(k_out, 16)

            with sp.Fori(3, 5) as pair:
                for par in range(2):
                    load_x(pair * 2 + par, par)
            sp.wait_ge(k_ready, 1)
            store_toep(0)
            with sp.Fori(5, G // 2) as pair:
                for par in range(2):
                    load_x(pair * 2 + par, par)
            store_toep(1)

            def load_toep(slot):
                ring = slot % SLOTS
                for half in range(2):
                    src = toep_d[:, slot * SLOT_CHANS:(slot + 1) * SLOT_CHANS, :]
                    sp.dma_start(toep[half * HALF:(half + 1) * HALF, ring, :, :], src).then_inc(toep_in[ring], 16)

            sp.wait_ge(k_out, 16 * KB)
            sp.wait_ge(wf_split, 1)
            sp.wait_ge(p_done, G // B)
            for slot in range(SLOTS):
                load_toep(slot)

            sp.wait_ge(y_added, G)

            def load_weights(q):
                if q >= 2:
                    sp.wait_ge(wt_tr, q - 1)
                if q < FC1_BANKS:
                    k, m = q // (MB // 4), q % (MB // 4) * 4
                    src = fc1_w.rearrange("(m p) c -> p m c", p=P)[:, m:m + 4, k * P:(k + 1) * P]
                    dst = w_raw[:, q % 2, :].rearrange("p (m c) -> p m c", m=4)
                else:
                    m = (q - FC1_BANKS) * 2
                    src = fc2_w.rearrange("(k p) n -> p k n", p=P)[:, :, m * P:(m + 2) * P]
                    dst = w_raw[:, q % 2, :].rearrange("p (k n) -> p k n", k=KB)
                sp.dma_start(dst, src).then_inc(fc_in[q % 2], 16)

            for q in range(2):
                load_weights(q)
            for n in range(CONV_BANKS):
                slot = (n + 1) * BANK_CHANS // SLOT_CHANS - 1 + SLOTS
                if (n + 1) * BANK_CHANS % SLOT_CHANS == 0 and slot < C // SLOT_CHANS:
                    sp.wait_ge(conv_mm, n + 1)
                    load_toep(slot)
                q = weight_bank_at(n)
                if q is not None and q + 2 < WEIGHT_BANKS:
                    load_weights(q + 2)

            def step(i, par):
                if live(i - 2):
                    sp.wait_ge(out_done, i - 1)
                    sp.dma_start(dram_group(out_g, i - 2), tb[:, :, :]).then_inc(stored, 16)
                if live(i):
                    if isinstance(i, int) and i == 0:
                        sp.wait_ge(conv_added, CONV_BANKS)
                    sp.dma_start(xr[:, par, :, :], dram_group(x_g, i)).then_inc(xr_in[par], 16)

            sweep(sp, step, **STEPS)
            sp.wait_ge(stored, 16 * G)

        @block.gpsimd
        def _(pool):
            steps = [0]

            def alone(ins):
                steps[0] += 1
                ins.then_inc(tables_set, 1)
                pool.wait_ge(tables_set, steps[0])

            def count(t, pattern, base):
                alone(pool.iota(t, pattern=pattern, base=base, channel_multiplier=0, allow_small_or_imprecise_dtypes=True))

            alone(pool.memset(ones[:, :], 1.0))
            pool.affine_select(out=ident[:, :], in_=ones[:, :], compare_op=ALU.is_equal, fill=0.0, base=0,
                               pattern=[[-1, P]], channel_multiplier=1).then_inc(ident_set, 1)
            pool.wait_ge(ident_set, 1)
            alone(pool.memset(mhalf[:, :, :], -0.5))
            count(times[:, 0, :], [[1, P]], 0)
            count(times[:, 3, 0:G], [[P, G]], 0)
            count(times[top, 1, :], [[-1, P]], P - 1)
            count(times[bot, 1, 0:HALF], [[-1, HALF]], HALF - 1)
            count(times[top, 2, :], [[1, P]], 1)
            count(times[bot, 2, HALF:P], [[1, HALF]], 1)
            alone(pool.memset(decay[bot, 1, HALF:P], 0.0))
            alone(pool.memset(e_y[bot, 0:HALF], 0.0))
            alone(pool.memset(kpad[:, :, :], 0.0))
            alone(pool.memset(f_all[bot, :, :], 1.0))
            alone(pool.memset(st[top, 0, :, :], 0.0))
            alone(pool.memset(gk[:, :, :], 0.0))
            assert steps[0] == POOL_TABLES

            def step(t, par):
                first = isinstance(t, int) and t == -1

                def modulate():
                    if first:
                        pool.wait_ge(a_in, 32)
                    pool.wait_ge(z_done, t + 2)
                    pool.tensor_tensor(z[:, 1 - par, :, :], z[:, 1 - par, :, :], a_t[:, :, :], ALU.mult).then_inc(za_done, 1)

                if live(t + 1) and not first:
                    modulate()
                if live(t + 2) or live(t):
                    pool.wait_ge(ve_both, t + 3)
                    pool.tensor_tensor(rstd[:, par, kinds(t), :], ve[:, kinds(t), :], mhalf[:, kinds(t), :], ALU.pow) \
                        .then_inc(rstd_both, 1)
                if first:
                    modulate()
                if live(t + 1):
                    pool.wait_ge(za_done, t + 2)
                    pool.tensor_tensor(group(h, t + 1), z[:, 1 - par, :, :], sa_t[:, :, :], ALU.add).then_inc(h_done, 1)

            for t in range(-2, FIRST_STEPS["first"]):
                step(t, t % 2)
            sweep(pool, step, **FIRST_STEPS)

            def rsqrt(which, n, par):
                pool.wait_ge(ve_done[which], n)
                pool.tensor_tensor(rstd[:, par, which, :], ve[:, which, :], mhalf[:, which, :], ALU.pow) \
                    .then_inc(rstd_done[which], 1)

            pool.wait_ge(p_done, G // B)
            for n in range(CONV_BANKS):
                hc = h[:, :, :, conv_chans(n)]
                pool.wait_ge(conv_added, n + 1)
                pool.tensor_tensor(hc, hc, p_tab[:, :, conv_chans(n)].unsqueeze(2).to_broadcast([P, G, B, BANK_CHANS]),
                                   ALU.add).then_inc(p_added, 1)
            pool.wait_ge(gates_in, 48)

            def main(i, par):
                if live(i - 1):
                    pool.wait_ge(s2_done, i)
                    pool.wait_ge(xg_done, i)
                    pool.tensor_tensor(xr[:, 1 - par, :, :], s1[:, :, :], xr[:, 1 - par, :, :], ALU.add).then_inc(x2_done, 1)
                if live(i - 2):
                    pool.wait_ge(tanh_done, i - 1)
                    pool.tensor_tensor(tb[:, :, :], tb[:, :, :], gb_t[:, :, :], ALU.mult).then_inc(gated, 1)
                if live(i - 1):
                    rsqrt(1, i, 1 - par)
                if live(i + 1):
                    rsqrt(0, i + 2, 1 - par)
                if live(i):
                    if isinstance(i, int):
                        pool.wait_ge(xr_in[par], (i // 2 + 1) * 16)
                    elif par == 0:
                        pool.wait_ge(xr_in[0], i * 8 + 16)
                    else:
                        pool.wait_ge(xr_in[1], i * 8 + 8)
                    pool.tensor_tensor(xr[:, par, :, :], xr[:, par, :, :], gab2_t[:, :, :], ALU.add).then_inc(xg_done, 1)

            sweep(pool, main, **STEPS)

        @block.scalar
        def _(act):
            with nc.allow_non_contiguous_dma(reason="columns of a few hundred words, once"):
                for k in range(KB):
                    act.dma_start(condT[:, k, :], cond[:, k * P:(k + 1) * P].rearrange("b p -> p b")).then_inc(cond_in, 16)
                act.dma_start(logs[top, 0:1], log_tau.unsqueeze(1)).then_inc(logs_in, 16)
                act.dma_start(logs[bot, 0:1], log_tau.unsqueeze(1)).then_inc(logs_in, 16)
                act.dma_start(logs[:, 1:2], bass.AP(tensor=log_dt.tensor, offset=0, ap=[[0, P], [1, 1]])).then_inc(logs_in, 16)

            act.wait_ge(cond_in, 16 * KB)
            act.activation(sil[:, 0, :, :], condT[:, :, :], ACT.Exp, scale=-1.0).then_inc(cond_exp, 1)
            act.wait_ge(sp_step, 1)
            act.activation(spl[:, 1, :], spl[:, 0, :], ACT.Exp, scale=-1.0).then_inc(log_exp, 1)
            act.wait_ge(sp_step, N_SP)
            act.wait_ge(tables_set, POOL_TABLES)
            act.activation(decay[:, 0, :], times[:, 0, :], ACT.Exp, scale=nega[:, 0:1])
            act.activation(decay[top, 1, :], times[top, 1, :], ACT.Exp, scale=nega[top, 0:1])
            act.activation(decay[bot, 1, 0:HALF], times[bot, 1, 0:HALF], ACT.Exp, scale=nega[bot, 0:1])
            act.activation(decay[:, 2, 0:G], times[:, 3, 0:G], ACT.Exp, scale=nega[:, 0:1])
            act.activation(e_y[top, :], times[top, 2, :], ACT.Exp, scale=nega[top, 0:1])
            act.activation(e_y[bot, HALF:P], times[bot, 2, HALF:P], ACT.Exp, scale=nega[bot, 0:1]).then_inc(decay_done, 1)
            def normed(out_of, in_of, which, par, done):
                for b in range(B):
                    last = act.activation(out_of[:, b, :], in_of[:, b, :], ACT.Identity,
                                          bias=nmr[:, par, which, b:b + 1], scale=rstd[:, par, which, b:b + 1])
                last.then_inc(done, 1)

            def z_of(k, par):
                act.wait_ge(nmr_both, k + 1)
                if after(k - 2):
                    act.wait_ge(h_done, k - 1)
                normed(z[:, par, :, :], group(h, k), 0, par, z_done)

            def half_states_of(k, par):
                act.wait_ge(z_mm, k + 1)
                if after(k - 2):
                    act.wait_ge(y_mul, k - 1)
                act.copy(st[bot, par, :, :], z_bank(par)[bot, :, :]).then_inc(st_done, 1)

            def zh_of(k, par):
                act.wait_ge(nmr_both, k + 3)
                normed(group(zh, k), group(h, k), 1, par, zh_done)

            def step(t, par):
                if live(t - 2):
                    half_states_of(t - 2, par)
                if live(t + 2):
                    z_of(t + 2, par)
                if live(t):
                    zh_of(t, par)

            def times_table(r):
                act.wait_ge(p_mm, r + 1)
                act.copy(p_tab[:, r * B:(r + 1) * B, :], by_batch((fo, f1)[r % 2])).then_inc(p_done, 1)

            step(-2, 0)
            act.wait_ge(ffn_tr, 1)
            act.copy(wT[:, :, :, :].rearrange("p a k c -> p a (k c)"), fo).then_inc(ffn_trd, 1)
            step(-1, 1)
            act.wait_ge(sums_done, 1)
            act.wait_ge(tables_set, POOL_TABLES)
            for g in range(G):
                last = act.activation(f_all[top, g, :], f_first[:, :], ACT.Identity,
                                      bias=gk[:, 1, g:g + 1], scale=decay[top, 2, g:g + 1])
            last.then_inc(f_ready, 1)
            act.wait_ge(ffn_mm, 1)
            act.copy(m12[:, :, :].rearrange("p k c -> p (k c)"), f1[:, 0, :]).then_inc(m12_done, 1)
            act.wait_ge(mod_mm, 2)
            step(0, 0)
            act.wait_ge(ffn_mm, 2)
            act.copy(wf[:, :, :].rearrange("p k c -> p (k c)"), f1[:, 1, :]).then_inc(wf_done, 1)
            times_table(0)
            times_table(1)
            step(1, 1)
            for r in range(2, G // B):
                times_table(r)
            assert KB * NMOD * C >= 2 * B * C
            act.wait_ge(k_ready, 1)
            act.wait_ge(mod_out, 16)
            act.wait_ge(wf_split, 1)
            sweep(act, step, **FIRST_STEPS)

            act.wait_ge(y_added, G)
            for q, dst in enumerate(weight_banks(fc1_hi, fc2_hi)):
                act.wait_ge(wt_tr, q + 1)
                act.copy(dst, tr[:, q % 2, :]).then_inc(wt_hi, 1)

            act.wait_ge(conv_added, CONV_BANKS)

            def main(i, par):
                def gelu(m):
                    act.wait_ge(fc1_mm, i * MB + m + 1)
                    if m >= 2 or after(i - 1):
                        act.wait_ge(hid_split, i * MB + m - 1)
                    act.activation(gel[:, m % 2, :], f1[:, m % 2, :], ACT.Gelu, bias=fc1b_c[:, m:m + 1]).then_inc(gelu_done, 1)

                def channel_modulated(k):
                    for b in range(B):
                        last = act.activation(fT[:, k, b * P:(b + 1) * P], fo[:, k, b * P:(b + 1) * P], ACT.Identity,
                                              bias=sb_c[:, k, b:b + 1], scale=cb_c[:, k, b:b + 1])
                    last.then_inc(fT_done, 1)

                if live(i):
                    gelu(0)
                if live(i - 2):
                    act.wait_ge(fb_done, i - 1)
                    act.activation(tb[:, :, :], tb[:, :, :], ACT.Tanh).then_inc(tanh_done, 1)
                if live(i):
                    for m in range(1, 4):
                        gelu(m)
                if live(i - 1):
                    act.wait_ge(nmr_done[1], i)
                    normed(zf, xr[:, 1 - par, :, :], 1, 1 - par, zf_done)
                if live(i):
                    gelu(4)
                    gelu(5)
                if live(i + 1):
                    act.wait_ge(nmr_done[0], i + 2)
                    normed(zn, group(h, i + 1), 0, 1 - par, zn_done)
                if live(i):
                    gelu(6)
                if live(i - 1):
                    act.wait_ge(zf_tr, i)
                    if isinstance(i, int) and i == 1:
                        act.wait_ge(mod_columns_in, 16 * 2 * KB)
                    channel_modulated(0)
                if live(i):
                    gelu(7)
                if live(i - 1):
                    channel_modulated(1)
                if live(i + 1):
                    act.wait_ge(zn_tr, i + 2)
                    if isinstance(i, int) and i == -1:
                        act.wait_ge(columns_in, 64)
                    for k in range(KB):
                        last = act.activation(gT[:, k, :], tr[:, k, :], ACT.Identity,
                                              bias=n2b_c[:, k:k + 1], scale=n2w_c[:, k:k + 1])
                    last.then_inc(gT_done, 1)

            sweep(act, main, **STEPS)

        @block.vector
        def _(v):
            v.wait_ge(cond_exp, 1)
            v.tensor_scalar(sil[:, 0, :, :], sil[:, 0, :, :], 1.0, None, ALU.add).then_inc(sil_step, 1)
            v.wait_ge(sil_step, 1)
            v.reciprocal(sil[:, 1, :, :], sil[:, 0, :, :]).then_inc(sil_step, 1)
            v.wait_ge(sil_step, 2)
            v.tensor_tensor(sil[:, 0, :, :], sil[:, 1, :, :], condT[:, :, :], ALU.mult).then_inc(sil_step, 1)

            done = [0]

            def chain(ins):
                done[0] += 1
                ins.then_inc(sp_step, 1)
                v.wait_ge(sp_step, done[0])

            absx, y, den, s, s2, q, pos = (spl[:, i, :] for i in range(7))
            v.wait_ge(logs_in, 48)
            chain(v.scalar_tensor_tensor(absx, logs[:, :], -1.0, logs[:, :], ALU.mult, ALU.max))
            v.wait_ge(log_exp, 1)
            chain(v.tensor_scalar(den, y, 2.0, None, ALU.add))
            chain(v.reciprocal(s2, den))
            chain(v.tensor_tensor(s, y, s2, ALU.mult))
            chain(v.tensor_tensor(s2, s, s, ALU.mult))
            chain(v.tensor_scalar(q, s2, 1.0 / (2 * LOG1P_TERMS + 1), None, ALU.mult))
            for j in range(LOG1P_TERMS - 1, 0, -1):
                chain(v.scalar_tensor_tensor(q, q, 1.0 / (2 * j + 1), s2, ALU.add, ALU.mult))
            chain(v.scalar_tensor_tensor(q, q, 1.0, s, ALU.add, ALU.mult))
            chain(v.tensor_scalar(pos, logs[:, :], 0.0, None, ALU.max))
            chain(v.scalar_tensor_tensor(q, q, 2.0, pos, ALU.mult, ALU.add))
            chain(v.scalar_tensor_tensor(nega[:, 0:1], q[:, 0:1], -1.0, q[:, 1:2], ALU.mult, ALU.mult))

            steps = [0]

            def mod(ins):
                steps[0] += 1
                ins.then_inc(mod_step, 1)
                v.wait_ge(mod_step, steps[0])

            def mod_bank(i, r):
                return v.tensor_copy(modr[:, 2 * i:2 * i + 2, :].rearrange("b a c -> b (a c)"), r)

            v.wait_ge(mod_mm, 1)
            mod(mod_bank(0, acc[0:B, 0, :]))
            v.tensor_scalar(modr[:, CA, :], modr[:, CA, :], 1.0, None, ALU.add).then_inc(mod_a_rows, 1)
            v.wait_ge(mod_mm, 2)
            mod_bank(1, acc[0:B, 1, :])
            mod_bank(2, f1[0:B, 0, :]).then_inc(mod_copied, 1)

            def gate_rows():
                v.wait_ge(mod_copied, 1)
                v.tensor_scalar(modr[:, CB, :], modr[:, CB, :], 1.0, None, ALU.add)
                gates = modr[:, GA:GB + 1:GB - GA, :]
                sign, size = gtmp[:, 0, :, :], gtmp[:, 1, :, :]
                v.tensor_scalar(sign, gates, 0.0, 2.0, ALU.is_ge, ALU.mult)
                mod(v.scalar_tensor_tensor(size, gates, -1.0, gates, ALU.mult, ALU.max))
                mod(v.tensor_scalar(size, size, GATE_MIN, None, ALU.max))
                mod(v.scalar_tensor_tensor(gates, sign, -1.0, size, ALU.add, ALU.mult))
                v.wait_ge(b2_in, 16)
                v.tensor_tensor(modr[:, GAB2, :], modr[:, GA, :], b2r[:, :], ALU.mult).then_inc(mod_rows, 1)

            def aggregate(which, bn_sem, parts_sem, mv_sem, ve_sem, n):
                _, m0, s0, _, m1, s1_ = (bn[:, which, :, i] for i in range(6))
                both, apart, spread_ = (mv[:, i, which, :] for i in range(3))
                v.wait_ge(bn_sem, n)
                v.tensor_tensor(both, m0, m1, ALU.add)
                v.tensor_tensor(apart, m0, m1, ALU.subtract)
                v.scalar_tensor_tensor(spread_, s0, C * EPS, s1_, ALU.add, ALU.add).then_inc(parts_sem, 1)
                v.wait_ge(parts_sem, n)
                v.scalar_tensor_tensor(apart, apart, 0.25, apart, ALU.mult, ALU.mult).then_inc(mv_sem, 1)
                v.wait_ge(mv_sem, n)
                v.scalar_tensor_tensor(ve[:, which, :], spread_, 1.0 / C, apart, ALU.mult, ALU.add).then_inc(ve_sem, 1)

            def bn_of(src, which):
                for b in range(B):
                    last = v.bn_stats(bn[:, which, b, :], src[:, b, :])
                return last

            def step(t, par):
                if live(t + 2):
                    if isinstance(t, int):
                        v.wait_ge(x_in[par], 16 * ((t + 2) // 2 + 1))
                    elif par == 0:
                        v.wait_ge(x_in[0], t * 8 + 32)
                    else:
                        v.wait_ge(x_in[1], t * 8 + 24)
                    last = bn_of(group(h, t + 2), 0)
                if live(t):
                    v.wait_ge(h_done, t + 1)
                    last = bn_of(group(h, t), 1)
                if live(t + 2) or live(t):
                    last.then_inc(bn_both, 1)
                    aggregate(kinds(t), bn_both, parts_both, mv_both, ve_both, t + 3)
                if live(t - 2):
                    v.wait_ge(z_mm, t - 1)
                    if after(t - 3):
                        v.wait_ge(carried, t - 2)
                        v.wait_ge(y_mul, t - 2)
                    v.scalar_tensor_tensor(st[top, 1 - par, :, :], st[top, par, :, :], d_g[:, 0:1], z_bank(par)[top, :, :],
                                           ALU.mult, ALU.add).then_inc(carried, 1)
                if live(t - 3):
                    v.wait_ge(y_mm, t - 2)
                    v.tensor_tensor(group(h, t - 3), group(h, t - 3), by_batch(f1), ALU.add).then_inc(y_added, 1)
                if live(t + 2) or live(t):
                    v.wait_ge(rstd_both, t + 3)
                    v.scalar_tensor_tensor(nmr[:, par, kinds(t), :], mv[:, 0, kinds(t), :], -0.5, rstd[:, par, kinds(t), :],
                                           ALU.mult, ALU.mult).then_inc(nmr_both, 1)
                if live(t - 2):
                    v.wait_ge(st_done, t - 1)
                    if after(t - 4):
                        v.wait_ge(y_mm, t - 3)
                    v.tensor_tensor(ym[:, par, :, :], st[:, par, :, :], over_batches(mixw[:, :]), ALU.mult) \
                        .then_inc(y_mul, 1)

            v.wait_ge(decay_done, 1)
            v.tensor_tensor_scan(f_first[:, :], ones[top, :], decay[top, 0, :], 0.0, ALU.mult, ALU.add).then_inc(f_step, 1)
            v.wait_ge(f_step, 1)
            v.tensor_scalar(gk[:, 0, 0:G], decay[top, 2, 0:G], f_first[:, P - 1:P], None, ALU.mult).then_inc(f_step, 1)
            v.wait_ge(f_step, 2)
            v.tensor_tensor_scan(gk[:, 1, 1:G + 1], ones[top, 0:G], gk[:, 0, 0:G], 0.0, ALU.mult, ALU.add).then_inc(sums_done, 1)

            step(-2, 0)
            step(-1, 1)
            v.wait_ge(mix_tr, 1)
            v.wait_ge(norm1_in, 80)
            mixps = f1[:, 1, 0:C]
            v.tensor_tensor(mixw[:, :], mixps, n1w_t[:, :], ALU.mult)
            v.tensor_tensor(mixb[top, :], mixps[top, :], n1b_t[top, :], ALU.mult)
            v.tensor_tensor(mixb[HALF:HALF + 1, :], drow[HALF:HALF + 1, :], n1b_t[HALF:HALF + 1, :], ALU.mult).then_inc(mix_step, 1)
            v.wait_ge(wz_tr, 1)
            v.tensor_copy(w_z[:, :], tr[:, 0, 0:P]).then_inc(wz_done, 1)
            v.wait_ge(decay_done, 1)
            v.wait_ge(ident_set, 1)
            v.tensor_copy(d_g[:, :], decay[top, 2, 1:2]).then_inc(dg_done, 1)
            v.tensor_tensor(dcol[:, 0, :], dcol[:, 0, :], dcol[:, 1, :], ALU.mult).then_inc(k_step, 1)
            v.wait_ge(k_mm, 1)
            v.tensor_copy(kpad[:, :, HALF - 1:P - 1], tr[:, 1, 0:P].rearrange("p (k d) -> p k d", k=KB)).then_inc(k_step, 1)
            v.wait_ge(k_step, 2)
            v.tensor_tensor(kpad[:, :, HALF - 1], kpad[:, :, HALF - 1], dcol[:, 0, :], ALU.add).then_inc(k_ready, 1)
            step(0, 0)
            gate_rows()
            step(1, 1)
            v.wait_ge(wf_done, 1)
            v.tensor_copy(wf_hi[:, :, :], wf[:, :, :]).then_inc(f_step, 1)
            v.wait_ge(f_step, 3)
            v.tensor_tensor(wf_lo[:, :, :], wf[:, :, :], wf_hi[:, :, :].bitcast(F32), ALU.subtract).then_inc(wf_split, 1)

            sweep(v, step, **FIRST_STEPS)

            def statistics(src, which, n):
                bn_of(src, which).then_inc(bn_done[which], 1)
                aggregate(which, bn_done[which], parts_done[which], mv_done[which], ve_done[which], n)

            def shift(which, n, par):
                v.wait_ge(rstd_done[which], n)
                v.scalar_tensor_tensor(nmr[:, par, which, :], mv[:, 0, which, :], -0.5, rstd[:, par, which, :],
                                       ALU.mult, ALU.mult).then_inc(nmr_done[which], 1)

            def low_part(lo, whole, hi, done):
                v.tensor_tensor(lo, whole, hi.bitcast(F32), ALU.subtract).then_inc(done, 1)

            lows = weight_banks(fc1_lo, fc2_lo)
            highs = weight_banks(fc1_hi, fc2_hi)
            v.wait_ge(y_added, G)
            for n in range(CONV_BANKS):
                v.wait_ge(conv_mm, n + 1)
                hc = h[:, :, :, conv_chans(n)].rearrange("p g b c -> p (g b) c")
                bank = conv_bank(n).rearrange("p (c t) -> p t c", t=TILES)
                v.tensor_tensor(hc, hc, bank, ALU.add).then_inc(conv_added, 1)
                q = weight_bank_at(n)
                if q is not None:
                    v.wait_ge(wt_hi, q + 1)
                    low_part(lows[q], tr[:, q % 2, :], highs[q], wt_lo)

            def main(i, par):
                def split_hidden(m):
                    ring = m % HID_RING
                    v.wait_ge(gelu_done, i * MB + m + 1)
                    if m >= HID_RING or after(i - 1):
                        v.wait_ge(fc2_mm, i * MB + m + 1 - HID_RING)
                    v.tensor_copy(hid_hi[:, ring, :], gel[:, m % 2, :]).then_inc(hid_hi_done, 1)
                    v.wait_ge(hid_hi_done, i * MB + m + 1)
                    low_part(hid_lo[:, ring, :], gel[:, m % 2, :], hid_hi[:, ring, :], hid_split)

                if live(i - 1):
                    v.wait_ge(fc2_mm, i * MB)
                    if after(i - 2):
                        v.wait_ge(x2_done, i - 1)
                    v.tensor_tensor(s1[:, :, :], by_batch(acc), group(h, i - 1), ALU.add).then_inc(s1_done, 1)
                    v.wait_ge(s1_done, i)
                    v.tensor_tensor(s1[:, :, :], s1[:, :, :], ga_t[:, :, :], ALU.mult).then_inc(s2_done, 1)
                if live(i - 2):
                    v.wait_ge(f_mm, i - 1)
                    if after(i - 3):
                        v.wait_ge(stored, 16 * (i - 2))
                    v.tensor_tensor(tb[:, :, :], by_batch(fo), over_batches(fb_t[:, :]), ALU.add).then_inc(fb_done, 1)
                if live(i):
                    split_hidden(0)
                if live(i - 1):
                    v.wait_ge(x2_done, i)
                    statistics(xr[:, 1 - par, :, :], 1, i)
                if live(i):
                    split_hidden(1)
                if live(i - 2):
                    v.wait_ge(gated, i - 1)
                    v.tensor_tensor(tb[:, :, :], tb[:, :, :], xr[:, par, :, :], ALU.add).then_inc(out_done, 1)
                if live(i - 1):
                    shift(1, i, 1 - par)
                if live(i):
                    split_hidden(2)
                if live(i + 1):
                    statistics(group(h, i + 1), 0, i + 2)
                if live(i):
                    split_hidden(3)
                if live(i + 1):
                    shift(0, i + 2, 1 - par)
                if live(i):
                    for m in range(4, 8):
                        split_hidden(m)
                if live(i - 1):
                    v.wait_ge(fT_done, KB * i)
                    v.tensor_copy(f_hi[:, :, :], fT[:, :, :]).then_inc(f_hi_done, 1)
                    v.wait_ge(f_hi_done, i)
                    low_part(f_lo[:, :, :], fT[:, :, :], f_hi[:, :, :], f_split)
                if live(i + 1):
                    v.wait_ge(gT_done, i + 2)
                    if after(i):
                        v.wait_ge(fc1_mm, (i + 1) * MB)
                    v.tensor_copy(g_hi[:, :, :], gT[:, :, :]).then_inc(g_hi_done, 1)
                    v.wait_ge(g_hi_done, i + 2)
                    low_part(g_lo[:, :, :], gT[:, :, :], g_hi[:, :, :], g_split)

            v.wait_ge(p_added, CONV_BANKS)
            v.wait_ge(columns_in, 64)
            sweep(v, main, **STEPS)

        @block.tensor
        def _(pe):
            def mm(o, lhs, rhs, start, stop):
                return pe.matmul(o, lhs, rhs, start=start, stop=stop)

            pe.wait_ge(sil_step, 3)
            for i, bank in enumerate((acc[0:B, 0, :], acc[0:B, 1, :], f1[0:B, 0, :])):
                pe.wait_ge(wmod_in if i else wmod_a_in, 16)
                for k in range(KB):
                    last = mm(bank, sil[:, 0, k, :], wm[:, k, i * BANK:(i + 1) * BANK], k == 0, k == KB - 1)
                if i != 1:
                    last.then_inc(mod_mm, 1)
            pe.wait_ge(ident_set, 1)
            pe.wait_ge(mix_in, 32)
            for k in range(KB):
                last = pe.transpose(f1[:, 1, k * P:(k + 1) * P], mixn[:, k, :, :].rearrange("p a n -> p (a n)"), ident[:, :])
            last.then_inc(mix_tr, 1)
            pe.wait_ge(decay_done, 1)
            pe.transpose(tr[:, 0, 0:P], decay[:, 1, :], ident[:, :]).then_inc(wz_tr, 1)
            pe.wait_ge(ffn_in, 48)
            for i in range(2):
                for kc in range(KB):
                    for kd in range(KB):
                        last = pe.transpose(fo[:, i, kd * C + kc * P:kd * C + (kc + 1) * P],
                                            wn[:, i, kc, kd * P:(kd + 1) * P], ident[:, :])
            last.then_inc(ffn_tr, 1)
            pe.wait_ge(mix_step, 1)
            for k in range(KB):
                last = mm(tr[:, 1, k * HALF:(k + 1) * HALF], mixw[top, k * P:(k + 1) * P], decay[top, 0, 0:HALF], True, True)
            last.then_inc(k_mm, 1)
            pe.wait_ge(ffn_trd, 1)
            pe.wait_ge(mod_copied, 1)
            pe.wait_ge(mix_step, 1)
            for i, rhs in ((1, wn[:, 2, :, :]), (0, m12[:, :, :])):
                if i == 0:
                    pe.wait_ge(m12_done, 1)
                for r in range(KB):
                    for k in range(KB):
                        last = mm(f1[:, 1 - i, r * C:(r + 1) * C], wT[:, i, k, r * P:(r + 1) * P], rhs[:, k, :], k == 0, k == KB - 1)
                last.then_inc(ffn_mm, 1)
            def times_table(r):
                if r >= 2:
                    pe.wait_ge(p_done, r - 1)
                for b in range(B):
                    last = mm(by_batch((fo, f1)[r % 2])[:, b, :], f_all[0:HALF + 1, r * B + b, :], mixb[0:HALF + 1, :], True, True)
                last.then_inc(p_mm, 1)

            def states_of(k, par):
                pe.wait_ge(zh_done, k + 1)
                if after(k - 2):
                    pe.wait_ge(st_done, k - 1)
                    pe.wait_ge(carried, k - 1)
                for b in range(B):
                    last = mm(z_bank(par)[:, b, :], w_z[:, :], group(zh, k)[:, b, :], True, True)
                last.then_inc(z_mm, 1)

            def y_of(k, par):
                pe.wait_ge(y_mul, k + 1)
                if after(k - 1):
                    pe.wait_ge(y_added, k)
                else:
                    pe.wait_ge(p_done, G // B)
                for b in range(B):
                    last = mm(by_batch(f1)[:, b, :], e_y[:, :], ym[:, par, b, :], True, True)
                last.then_inc(y_mm, 1)

            def step(t, par):
                if live(t - 2):
                    y_of(t - 2, par)
                if live(t):
                    states_of(t, par)

            pe.wait_ge(f_ready, 1)
            for r in range(G // B):
                if r == 1:
                    pe.wait_ge(wf_done, 1)
                times_table(r)
            pe.wait_ge(k_ready, 1)
            step(0, 0)
            step(1, 1)
            sweep(pe, step, **dict(FIRST_STEPS, last=G))

            def transpose_weights(q):
                pe.wait_ge(fc_in[q % 2], 16 * (q // 2 + 1))
                if q >= 2:
                    pe.wait_ge(wt_lo, q - 1)
                for j in range(4):
                    to = j if q < FC1_BANKS else j % 2 * 2 + j // 2
                    last = pe.transpose(tr[:, q % 2, to * P:(to + 1) * P], w_raw[:, q % 2, j * P:(j + 1) * P], ident[:, :])
                last.then_inc(wt_tr, 1)

            def convolve(n):
                if n >= len(CONV_RING):
                    pe.wait_ge(conv_added, n + 1 - len(CONV_RING))
                for c in range(n * BANK_CHANS, (n + 1) * BANK_CHANS):
                    ring, place = c // SLOT_CHANS % SLOTS, c % SLOT_CHANS
                    if place == 0:
                        pe.wait_ge(toep_in[ring], 32 * (c // SLOT_CHANS // SLOTS + 1))
                    col = c % BANK_CHANS * TILES
                    for half in (top, bot):
                        last = mm(conv_bank(n)[half, col:col + TILES], toep[half, ring, place, :],
                                  zh[half, :, :, c].rearrange("p g b -> p (g b)"), True, True)
                last.then_inc(conv_mm, 1)

            convolve(0)
            convolve(1)
            y_of(G - 1, (G - 1) % 2)
            for n in range(2, CONV_BANKS):
                if n == 4:
                    pe.wait_ge(y_added, G)
                convolve(n)
                if weight_bank_at(n) is not None:
                    transpose_weights(weight_bank_at(n))

            def transposes(dst, src, ready, n, done):
                pe.wait_ge(ready, n)
                for k in range(KB):
                    for b in range(B):
                        last = pe.transpose(dst[:, k, b * P:(b + 1) * P], src[:, b, k * P:(k + 1) * P], ident[:, :])
                last.then_inc(done, 1)

            def main(i, par):
                def fc1(m):
                    if m == 0:
                        pe.wait_ge(g_split, i + 1)
                    if m >= 2 or after(i - 1):
                        pe.wait_ge(gelu_done, i * MB + m - 1)
                    terms = [(w, g, k) for k in range(KB) for w, g in ((fc1_hi, g_hi), (fc1_hi, g_lo), (fc1_lo, g_hi))]
                    for n, (w, g, k) in enumerate(terms):
                        last = mm(f1[:, m % 2, :], w[:, k, m * P:(m + 1) * P], g[:, k, :], n == 0, n == len(terms) - 1)
                    last.then_inc(fc1_mm, 1)

                def fc2(m):
                    ring = m % HID_RING
                    pe.wait_ge(hid_split, i * MB + m + 1)
                    if m == 0 and after(i - 1):
                        pe.wait_ge(s1_done, i)
                    for b in range(B):
                        for n, (w, g) in enumerate(((fc2_hi, hid_hi), (fc2_lo, hid_hi), (fc2_hi, hid_lo))):
                            last = pe.matmul(by_batch(acc)[:, b, :], g[:, ring, b * P:(b + 1) * P], w[:, m, :],
                                             start=m == 0 and n == 0 and b % 2 == 0, stop=m == MB - 1 and n == 2,
                                             skip_group_check=True)
                    last.then_inc(fc2_mm, 1)

                if live(i):
                    for m in range(6):
                        fc1(m)
                        if m >= FC2_LAG:
                            fc2(m - FC2_LAG)
                if live(i - 1):
                    if after(i - 2):
                        pe.wait_ge(fb_done, i - 1)
                    transposes(fo, zf, zf_done, i, zf_tr)
                if live(i):
                    for m in range(6, MB):
                        fc1(m)
                        fc2(m - FC2_LAG)
                if live(i + 1):
                    if after(i):
                        pe.wait_ge(gT_done, i + 1)
                    transposes(tr, zn, zn_done, i + 2, zn_tr)
                if live(i):
                    for m in range(MB - FC2_LAG, MB):
                        fc2(m)
                if live(i - 1):
                    pe.wait_ge(f_split, i)
                    for b in range(B):
                        terms = [(g, w, k) for k in range(KB) for g, w in ((f_hi, wf_hi), (f_hi, wf_lo), (f_lo, wf_hi))]
                        for n, (g, w, k) in enumerate(terms):
                            last = mm(by_batch(fo)[:, b, :], g[:, k, b * P:(b + 1) * P], w[:, k, :], n == 0, n == len(terms) - 1)
                    last.then_inc(f_mm, 1)

            pe.wait_ge(conv_added, CONV_BANKS)
            pe.wait_ge(wt_lo, WEIGHT_BANKS)
            sweep(pe, main, **STEPS)


_INS = ["L0_attn_x", "L0_attn_log_tau", "L0_attn_log_dt", "L0_attn_mix", "L0_attn_D", "L0_attn_norm1_w", "L0_attn_norm1_b",
        "L0_attn_norm2_w", "L0_attn_norm2_b", "L0_attn_fc1_w", "L0_attn_fc1_b", "L0_attn_fc2_w", "L0_attn_fc2_b",
        "L0_ffn_weight", "L0_ffn_aux_weight1", "L0_ffn_aux_weight2", "L0_ffn_bias", "L0_c", "L0_wmod"]


def kernel(**inputs):
    import numpy as _np
    import concourse.bacc as _bacc
    from concourse import mybir as _mybir
    from concourse.bass_utils import run_bass_kernel_spmd as _run

    nc = _bacc.Bacc("TRN2", target_bir_lowering=False, num_devices=1)
    arrays, args = {}, []
    for name in _INS:
        a = _np.ascontiguousarray(inputs[name])
        if a.ndim == 0:
            a = a.reshape(1)
        arrays[f"in_{name}_dram"] = a
        args.append(nc.dram_tensor(f"in_{name}_dram", a.shape, _mybir.dt.from_np(a.dtype), kind="ExternalInput").ap())
    shape = inputs["L0_attn_x"].shape
    args.append(nc.dram_tensor("out_0_dram", shape, _mybir.dt.float32, kind="ExternalOutput").ap())
    adaln_block(nc, *args)
    r = _run(nc, [arrays], core_ids=[0])
    return r.results[0]["out_0_dram"]
```

```python
from contextlib import ExitStack

import concourse.bass as bass
from concourse import mybir

F32 = mybir.dt.float32
F32R = mybir.dt.float32r
ALU = mybir.AluOpType
ACT = mybir.ActivationFunctionType

P = 128
BANK = 512
EPS = 1e-5
GATE_MIN = 0.25
LOG1P_TERMS = 9
FC2_LAG = 3
HID_RING = 4
SLOT_CHANS = 16
SLOTS = 2


def adaln_block(nc, x, log_tau, log_dt, mix, D, n1w, n1b, n2w, n2b, fc1_w, fc1_b, fc2_w, fc2_b,
                w0, w1, w2, fbias, cond, wmod, out):
    B, T, C = x.shape
    N = mix.shape[1]
    HID = fc1_w.shape[0]
    G = T // P
    KB = C // P
    MB = HID // P
    HALF = P // 2
    TILES = G * B
    NMOD = wmod.shape[1] // C
    MOD_BANKS = NMOD * C // BANK
    SA, CA, GA, SB, CB, GB, GAB2 = range(NMOD + 1)
    BANK_CHANS = BANK // TILES
    CONV_BANKS = C // BANK_CHANS
    assert N == HALF and B * C == 2 * BANK and KB == 2 and G % 4 == 0 and 2 * HALF == P

    top = slice(0, HALF)
    bot = slice(HALF, P)

    with ExitStack() as ctx:
        def tile(stack, name, shape, dt=F32, side="left"):
            return stack.enter_context(nc.sbuf_tensor(name, shape, dt, side=side))

        def sem(name):
            return ctx.enter_context(nc.semaphore(name))

        h = tile(ctx, "h", [P, G, B, C])
        p_tab = tile(ctx, "p_tab", [P, G, C])
        ga_t = tile(ctx, "ga_t", [P, B, C])
        gb_t = tile(ctx, "gb_t", [P, B, C])
        gab2_t = tile(ctx, "gab2_t", [P, B, C])
        fb_t = tile(ctx, "fb_t", [P, C])
        ident = tile(ctx, "ident", [P, P])
        n2w_c = tile(ctx, "n2w_c", [P, KB])
        n2b_c = tile(ctx, "n2b_c", [P, KB])
        fc1b_c = tile(ctx, "fc1b_c", [P, MB])
        cb_c = tile(ctx, "cb_c", [P, KB, B])
        sb_c = tile(ctx, "sb_c", [P, KB, B])
        mhalf = tile(ctx, "mhalf", [P, 2, B])
        bn = tile(ctx, "bn", [P, 2, B, 6])
        mv = tile(ctx, "mv", [P, 3, 2, B])
        ve = tile(ctx, "ve", [P, 2, B])
        rstd = tile(ctx, "rstd", [P, 2, 2, B])
        nmr = tile(ctx, "nmr", [P, 2, 2, B])
        wf_hi = tile(ctx, "wf_hi", [P, KB, C], F32R)
        wf_lo = tile(ctx, "wf_lo", [P, KB, C], F32R)

        setup = ExitStack()
        wm = tile(setup, "wm", [P, KB, NMOD * C])
        condT = tile(setup, "condT", [P, KB, B])
        sil = tile(setup, "sil", [P, 2, KB, B])
        logs = tile(setup, "logs", [P, 2])
        spl = tile(setup, "spl", [P, 7, 2])
        nega = tile(setup, "nega", [P, 1])
        mixn = tile(setup, "mixn", [P, KB, 2, N])
        n1w_t = tile(setup, "n1w_t", [P, C])
        n1b_t = tile(setup, "n1b_t", [P, C])
        dcol = tile(setup, "dcol", [P, 2, KB])
        drow = tile(setup, "drow", [P, C])
        times = tile(setup, "times", [P, 4, P])
        decay = tile(setup, "decay", [P, 3, P])
        ones = tile(setup, "ones", [P, P])
        f_first = tile(setup, "f_first", [HALF, P])
        gk = tile(setup, "gk", [HALF, 2, G + 1])
        modr = tile(setup, "modr", [B, NMOD + 1, C])
        gtmp = tile(setup, "gtmp", [B, 2, 2, C])
        b2r = tile(setup, "b2r", [B, C])
        mixb = tile(setup, "mixb", [P, C])
        f_all = tile(setup, "f_all", [P, G, P])
        wn = tile(setup, "wn", [P, 3, KB, C])
        wT = tile(setup, "wT", [P, 2, KB, C])
        m12 = tile(setup, "m12", [P, KB, C])
        wf = tile(setup, "wf", [P, KB, C])
        setup.close()
        conv = ExitStack()
        zh = tile(conv, "zh", [P, G, B, C])
        toep = tile(conv, "toep", [P, SLOTS, SLOT_CHANS, HALF])

        early = ExitStack()
        z = tile(early, "z", [P, 2, B, C], side="right")
        a_t = tile(early, "a_t", [P, B, C], side="right")
        sa_t = tile(early, "sa_t", [P, B, C], side="right")
        st = tile(early, "st", [P, 2, B, C], side="right")
        ym = tile(early, "ym", [P, 2, B, C], side="right")
        mixw = tile(early, "mixw", [P, C], side="right")
        w_z = tile(early, "w_z", [P, P], side="right")
        e_y = tile(early, "e_y", [P, P], side="right")
        d_g = tile(early, "d_g", [HALF, 1], side="right")
        kpad = tile(early, "kpad", [P, KB, P - 1], side="right")
        early.close()

        fc1_hi = tile(ctx, "fc1_hi", [P, KB, HID], F32R, side="right")
        fc1_lo = tile(ctx, "fc1_lo", [P, KB, HID], F32R, side="right")
        fc2_hi = tile(ctx, "fc2_hi", [P, MB, C], F32R, side="right")
        fc2_lo = tile(ctx, "fc2_lo", [P, MB, C], F32R, side="right")
        raw = ExitStack()
        w_raw = tile(raw, "w_raw", [P, 2, BANK], side="right")
        raw.close()
        conv.close()

        xr = tile(ctx, "xr", [P, 2, B, C])
        s1 = tile(ctx, "s1", [P, B, C])
        zn = tile(ctx, "zn", [P, B, C])
        zf = tile(ctx, "zf", [P, B, C])
        tb = tile(ctx, "tb", [P, B, C])
        gT = tile(ctx, "gT", [P, KB, BANK])
        g_hi = tile(ctx, "g_hi", [P, KB, BANK], F32R)
        g_lo = tile(ctx, "g_lo", [P, KB, BANK], F32R)
        fT = tile(ctx, "fT", [P, KB, BANK])
        f_hi = tile(ctx, "f_hi", [P, KB, BANK], F32R)
        f_lo = tile(ctx, "f_lo", [P, KB, BANK], F32R)
        gel = tile(ctx, "gel", [P, 2, BANK])
        hid_hi = tile(ctx, "hid_hi", [P, HID_RING, BANK], F32R)
        hid_lo = tile(ctx, "hid_lo", [P, HID_RING, BANK], F32R)

        ps = ctx.enter_context(nc.psum_tensor("ps", [P, 8, BANK], F32))
        acc, f1, tr, fo = (ps[:, 2 * i:2 * i + 2, :] for i in range(4))

        def by_batch(pair):
            return pair.rearrange("p a n -> p (a n)").rearrange("p (b c) -> p b c", c=C)

        mod_d = nc.dram_tensor("mod_d", (B, NMOD + 1, C), F32, kind="Internal").ap()
        toep_d = nc.dram_tensor("toep_d", (HALF, C, HALF), F32, kind="Internal").ap()
        x_g = x.rearrange("b (g p) c -> g p b c", p=P)
        out_g = out.rearrange("b (g p) c -> g p b c", p=P)

        cond_in, logs_in, wmod_in, mix_in, norm1_in = sem("cond_in"), sem("logs_in"), sem("wmod_in"), sem("mix_in"), sem("norm1_in")
        b2_in, ffn_in, columns_in, mod_out, k_out = sem("b2_in"), sem("ffn_in"), sem("columns_in"), sem("mod_out"), sem("k_out")
        a_in, gates_in, mod_columns_in = sem("a_in"), sem("gates_in"), sem("mod_columns_in")
        x_in = [sem("x_in0"), sem("x_in1")]
        toep_in = [sem(f"toep_in{s}") for s in range(SLOTS)]
        fc_in = [sem("fc_in0"), sem("fc_in1")]
        xr_in, stored = [sem("xr_in0"), sem("xr_in1")], sem("stored")
        tables_set, ident_set = sem("tables_set"), sem("ident_set")
        cond_exp, sil_step, log_exp, sp_step = sem("cond_exp"), sem("sil_step"), sem("log_exp"), sem("sp_step")
        mod_mm, mod_step, mod_copied, mod_a_rows, mod_rows = (sem("mod_mm"), sem("mod_step"), sem("mod_copied"),
                                                              sem("mod_a_rows"), sem("mod_rows"))
        wmod_a_in, mod_a_out = sem("wmod_a_in"), sem("mod_a_out")
        decay_done, mix_tr, mix_step, wz_tr, wz_done, dg_done = (sem("decay_done"), sem("mix_tr"), sem("mix_step"),
                                                                 sem("wz_tr"), sem("wz_done"), sem("dg_done"))
        k_mm, k_step, k_ready = sem("k_mm"), sem("k_step"), sem("k_ready")
        f_step, sums_done, f_ready, p_mm, p_done = sem("f_step"), sem("sums_done"), sem("f_ready"), sem("p_mm"), sem("p_done")
        ffn_tr, ffn_trd, ffn_mm, m12_done, wf_done, wf_split = (sem("ffn_tr"), sem("ffn_trd"), sem("ffn_mm"), sem("m12_done"),
                                                                sem("wf_done"), sem("wf_split"))
        bn_both, parts_both, mv_both, ve_both, rstd_both, nmr_both = (
            sem("bn_both"), sem("parts_both"), sem("mv_both"), sem("ve_both"), sem("rstd_both"), sem("nmr_both"))
        bn_done = [sem("bn_x1"), sem("bn_x2")]
        parts_done = [sem("parts_x1"), sem("parts_x2")]
        mv_done = [sem("mv_x1"), sem("mv_x2")]
        ve_done = [sem("ve_x1"), sem("ve_x2")]
        rstd_done = [sem("rstd_x1"), sem("rstd_x2")]
        nmr_done = [sem("nmr_x1"), sem("nmr_x2")]
        z_done, za_done, h_done, zh_done = sem("z_done"), sem("za_done"), sem("h_done"), sem("zh_done")
        z_mm, st_done, carried, y_mul, y_mm, y_added = sem("z_mm"), sem("st_done"), sem("carried"), sem("y_mul"), sem("y_mm"), sem("y_added")
        conv_mm, conv_added, p_added = sem("conv_mm"), sem("conv_added"), sem("p_added")
        wt_tr, wt_hi, wt_lo = sem("wt_tr"), sem("wt_hi"), sem("wt_lo")
        zn_done, zn_tr, gT_done, g_split = sem("zn_done"), sem("zn_tr"), sem("gT_done"), sem("g_split")
        fc1_mm, gelu_done, hid_split, fc2_mm = sem("fc1_mm"), sem("gelu_done"), sem("hid_split"), sem("fc2_mm")
        g_hi_done, hid_hi_done, f_hi_done = sem("g_hi_done"), sem("hid_hi_done"), sem("f_hi_done")
        s1_done, s2_done, xg_done, x2_done = sem("s1_done"), sem("s2_done"), sem("xg_done"), sem("x2_done")
        zf_done, zf_tr, fT_done, f_split, f_mm = sem("zf_done"), sem("zf_tr"), sem("fT_done"), sem("f_split"), sem("f_mm")
        fb_done, tanh_done, gated, out_done = sem("fb_done"), sem("tanh_done"), sem("gated"), sem("out_done")

        def live(k):
            return not isinstance(k, int) or 0 <= k < G

        def after(k):
            return not isinstance(k, int) or k >= 0

        def sweep(eng, step, first, last, full_from, full_to):
            for t in range(first, full_from):
                step(t, t % 2)
            with eng.Fori(full_from // 2, (full_to + 1) // 2) as pair:
                for par in range(2):
                    step(pair * 2 + par, par)
            for t in range(full_to + 1, last + 1):
                step(t, t % 2)

        def kinds(t):
            return slice(0 if live(t + 2) else 1, 2 if live(t) else 1)

        FIRST_STEPS = dict(first=2, last=G + 2, full_from=4, full_to=G - 3)
        STEPS = dict(first=-1, last=G + 1, full_from=2, full_to=G - 3)

        def pieces(k):
            return enumerate([slice(0, B // 2), slice(B // 2, B)] if isinstance(k, int) and k == G - 1 else [slice(0, B)])

        def latest(i):
            return isinstance(i, int) and i == G

        def tb_of(k):
            return zn if isinstance(k, int) and k == G - 1 else tb

        def by_parts(n):
            return [slice(0, 1), slice(1, G)] if n == CONV_BANKS - 1 else [slice(0, G)]

        LAST_PIECE = 1

        def group(t, k):
            return t[:, k, :, :] if isinstance(k, int) else t[:, bass.ds(k, 1), :, :].rearrange("p o b c -> p (o b) c")

        def dram_group(t, k):
            return t[k, :, :, :] if isinstance(k, int) else t[bass.ds(k, 1), :, :, :].rearrange("o p b c -> (o p) b c")

        def conv_chans(n):
            return slice(n * BANK_CHANS, (n + 1) * BANK_CHANS)

        CONV_RING = (6, 7, 0, 1, 2, 3)

        def conv_bank(n):
            return ps[:, CONV_RING[n % len(CONV_RING)], :]

        def zfT_block(group_, k, b):
            if isinstance(group_, int) and group_ == G - 1:
                piece, place = b // (B // 2), k * (B // 2) + b % (B // 2)
                return tr[:, piece, place * P:(place + 1) * P]
            return fo[:, k, b * P:(b + 1) * P]

        def z_bank(par):
            return by_batch((acc, tr)[par])

        def over_batches(t):
            return t.unsqueeze(1).to_broadcast([P, B, C])

        def column(v):
            return v.rearrange("(k p) -> p k", p=P)

        def spread(v, parts):
            return v.unsqueeze(0).to_broadcast([parts, v.shape[0]])

        POOL_TABLES = 14
        N_SP = LOG1P_TERMS + 9
        FC1_BANKS = KB * HID // BANK
        WEIGHT_BANKS = FC1_BANKS + MB * C // BANK
        assert 2 * WEIGHT_BANKS + 4 <= CONV_BANKS

        def weight_bank_at(n):
            return n // 2 - 2 if n % 2 and 1 < n // 2 <= WEIGHT_BANKS + 1 else None

        block = ctx.enter_context(nc.Block())

        def weight_banks(fc1, fc2):
            banks = [fc1[:, k, q * BANK:(q + 1) * BANK] for k in range(KB) for q in range(HID // BANK)]
            return banks + [fc2[:, 2 * q:2 * q + 2, :].rearrange("p m c -> p (m c)") for q in range(MB // 2)]

        @block.sync
        def _(sp):
            def load_x(k, par):
                if not isinstance(k, int):
                    sp.wait_ge(x_in[par], (k - par) * 8)
                elif k >= 2:
                    sp.wait_ge(x_in[par], k // 2 * 16)
                sp.dma_start(group(h, k), dram_group(x_g, k)).then_inc(x_in[par], 16)

            with nc.allow_non_contiguous_dma(reason="columns of a few hundred words, once"):
                w = wmod.rearrange("(k p) n -> p k n", p=P)
                sp.dma_start(wm[:, :, 0:BANK], w[:, :, 0:BANK]).then_inc(wmod_a_in, 16)
                for dup in range(2):
                    sp.dma_start(mixn[:, :, dup, :], mix.rearrange("(k p) n -> p k n", p=P)).then_inc(mix_in, 16)
                sp.dma_start(wm[:, :, BANK:NMOD * C], w[:, :, BANK:NMOD * C]).then_inc(wmod_in, 16)
                load_x(0, 0)
                load_x(1, 1)
                sp.dma_start(n1w_t[:, :], spread(n1w, P)).then_inc(norm1_in, 16)
                sp.dma_start(n1b_t[:, :], spread(n1b, P)).then_inc(norm1_in, 16)
                sp.dma_start(dcol[:, 0, :], column(D)).then_inc(norm1_in, 16)
                sp.dma_start(dcol[:, 1, :], column(n1w)).then_inc(norm1_in, 16)
                sp.dma_start(drow[HALF:HALF + 1, :], spread(D, 1)).then_inc(norm1_in, 16)

            for i, w in enumerate((w0, w1, w2)):
                sp.dma_start(wn[:, i, :, :], w.rearrange("(k p) n -> p k n", p=P)).then_inc(ffn_in, 16)
            load_x(2, 0)
            load_x(3, 1)

            def columns():
                sp.dma_start(b2r[:, :], spread(fc2_b, B)).then_inc(b2_in, 16)
                sp.dma_start(fb_t[:, :], spread(fbias, P)).then_inc(columns_in, 16)
                with nc.allow_non_contiguous_dma(reason="columns of a few hundred words, once"):
                    sp.dma_start(n2w_c[:, :], column(n2w)).then_inc(columns_in, 16)
                    sp.dma_start(n2b_c[:, :], column(n2b)).then_inc(columns_in, 16)
                    sp.dma_start(fc1b_c[:, :], column(fc1_b)).then_inc(columns_in, 16)

            def rows(q, t, s):
                src = bass.AP(tensor=mod_d.tensor, offset=q * C, ap=[[0, P], [(NMOD + 1) * C, B], [1, C]])
                sp.dma_start(t[:, :, :], src).then_inc(s, 16)

            sp.wait_ge(mod_a_rows, 1)
            sp.dma_start(mod_d[:, 0:GA, :], modr[:, 0:GA, :]).then_inc(mod_a_out, 16)
            sp.wait_ge(mod_a_out, 16)
            rows(CA, a_t, a_in)
            rows(SA, sa_t, a_in)
            columns()
            for k in range(4, 6):
                load_x(k, k % 2)
            sp.wait_ge(mod_rows, 1)
            sp.dma_start(mod_d[:, GA:NMOD + 1, :], modr[:, GA:NMOD + 1, :]).then_inc(mod_out, 16)
            sp.wait_ge(mod_out, 16)
            for q, t in ((GA, ga_t), (GB, gb_t), (GAB2, gab2_t)):
                rows(q, t, gates_in)
            with nc.allow_non_contiguous_dma(reason="a few hundred words, once"):
                for q, t in ((CB, cb_c), (SB, sb_c)):
                    for k in range(KB):
                        src = bass.AP(tensor=mod_d.tensor, offset=q * C + k * P, ap=[[1, P], [(NMOD + 1) * C, B]])
                        sp.dma_start(t[:, k, :], src).then_inc(mod_columns_in, 16)

            def store_toep(k):
                row = kpad[:, k, :]
                src = bass.AP(tensor=row.tensor, offset=row.offset + HALF - 1, ap=[row.ap[0], [-1, HALF], [1, HALF]])
                sp.dma_start(toep_d[:, k * P:(k + 1) * P, :].rearrange("s c t -> c s t"), src).then_inc(k_out, 16)

            with sp.Fori(3, 5) as pair:
                for par in range(2):
                    load_x(pair * 2 + par, par)
            sp.wait_ge(k_ready, 1)
            store_toep(0)
            with sp.Fori(5, G // 2) as pair:
                for par in range(2):
                    load_x(pair * 2 + par, par)
            store_toep(1)

            def load_toep(slot):
                ring = slot % SLOTS
                for half in range(2):
                    src = toep_d[:, slot * SLOT_CHANS:(slot + 1) * SLOT_CHANS, :]
                    sp.dma_start(toep[half * HALF:(half + 1) * HALF, ring, :, :], src).then_inc(toep_in[ring], 16)

            sp.wait_ge(k_out, 16 * KB)
            sp.wait_ge(wf_split, 1)
            sp.wait_ge(p_done, G // B)
            for slot in range(SLOTS):
                load_toep(slot)

            sp.wait_ge(y_added, G)

            def load_weights(q):
                if q >= 2:
                    sp.wait_ge(wt_tr, q - 1)
                if q < FC1_BANKS:
                    k, m = q // (MB // 4), q % (MB // 4) * 4
                    src = fc1_w.rearrange("(m p) c -> p m c", p=P)[:, m:m + 4, k * P:(k + 1) * P]
                    dst = w_raw[:, q % 2, :].rearrange("p (m c) -> p m c", m=4)
                else:
                    m = (q - FC1_BANKS) * 2
                    src = fc2_w.rearrange("(k p) n -> p k n", p=P)[:, :, m * P:(m + 2) * P]
                    dst = w_raw[:, q % 2, :].rearrange("p (k n) -> p k n", k=KB)
                sp.dma_start(dst, src).then_inc(fc_in[q % 2], 16)

            for q in range(2):
                load_weights(q)
            for n in range(CONV_BANKS):
                slot = (n + 1) * BANK_CHANS // SLOT_CHANS - 1 + SLOTS
                if (n + 1) * BANK_CHANS % SLOT_CHANS == 0 and slot < C // SLOT_CHANS:
                    sp.wait_ge(conv_mm, n + 1)
                    load_toep(slot)
                q = weight_bank_at(n)
                if q is not None and q + 2 < WEIGHT_BANKS:
                    load_weights(q + 2)

            def step(i, par):
                if live(i - 2):
                    for p, bs in pieces(i - 2):
                        sp.wait_ge(out_done, i - 1 + p)
                        sp.dma_start(dram_group(out_g, i - 2)[:, bs, :], tb_of(i - 2)[:, bs, :]).then_inc(stored, 16)
                if live(i):
                    if isinstance(i, int) and i == 0:
                        sp.wait_ge(conv_added, CONV_BANKS)
                    sp.dma_start(xr[:, par, :, :], dram_group(x_g, i)).then_inc(xr_in[par], 16)

            sweep(sp, step, **STEPS)
            sp.wait_ge(stored, 16 * (G + LAST_PIECE))

        @block.gpsimd
        def _(pool):
            steps = [0]

            def alone(ins):
                steps[0] += 1
                ins.then_inc(tables_set, 1)
                pool.wait_ge(tables_set, steps[0])

            def count(t, pattern, base):
                alone(pool.iota(t, pattern=pattern, base=base, channel_multiplier=0, allow_small_or_imprecise_dtypes=True))

            alone(pool.memset(ones[:, :], 1.0))
            pool.affine_select(out=ident[:, :], in_=ones[:, :], compare_op=ALU.is_equal, fill=0.0, base=0,
                               pattern=[[-1, P]], channel_multiplier=1).then_inc(ident_set, 1)
            pool.wait_ge(ident_set, 1)
            alone(pool.memset(mhalf[:, :, :], -0.5))
            count(times[:, 0, :], [[1, P]], 0)
            count(times[:, 3, 0:G], [[P, G]], 0)
            count(times[top, 1, :], [[-1, P]], P - 1)
            count(times[bot, 1, 0:HALF], [[-1, HALF]], HALF - 1)
            count(times[top, 2, :], [[1, P]], 1)
            count(times[bot, 2, HALF:P], [[1, HALF]], 1)
            alone(pool.memset(decay[bot, 1, HALF:P], 0.0))
            alone(pool.memset(e_y[bot, 0:HALF], 0.0))
            alone(pool.memset(kpad[:, :, :], 0.0))
            alone(pool.memset(f_all[bot, :, :], 1.0))
            alone(pool.memset(st[top, 0, :, :], 0.0))
            alone(pool.memset(gk[:, :, :], 0.0))
            assert steps[0] == POOL_TABLES

            def step(t, par):
                first = isinstance(t, int) and t == -1

                def modulate():
                    if first:
                        pool.wait_ge(a_in, 32)
                    pool.wait_ge(z_done, t + 2)
                    pool.tensor_tensor(z[:, 1 - par, :, :], z[:, 1 - par, :, :], a_t[:, :, :], ALU.mult).then_inc(za_done, 1)

                if live(t + 1) and not first:
                    modulate()
                if live(t + 2) or live(t):
                    pool.wait_ge(ve_both, t + 3)
                    pool.tensor_tensor(rstd[:, par, kinds(t), :], ve[:, kinds(t), :], mhalf[:, kinds(t), :], ALU.pow) \
                        .then_inc(rstd_both, 1)
                if first:
                    modulate()
                if live(t + 1):
                    pool.wait_ge(za_done, t + 2)
                    pool.tensor_tensor(group(h, t + 1), z[:, 1 - par, :, :], sa_t[:, :, :], ALU.add).then_inc(h_done, 1)

            for t in range(-2, FIRST_STEPS["first"]):
                step(t, t % 2)
            sweep(pool, step, **FIRST_STEPS)

            def rsqrt(which, n, par, bs=slice(0, B)):
                pool.wait_ge(ve_done[which], n)
                pool.tensor_tensor(rstd[:, par, which, bs], ve[:, which, bs], mhalf[:, which, bs], ALU.pow) \
                    .then_inc(rstd_done[which], 1)

            pool.wait_ge(p_done, G // B)
            for n in range(CONV_BANKS):
                for part, gs in enumerate(by_parts(n)):
                    hc = h[:, gs, :, conv_chans(n)]
                    pc = p_tab[:, gs, conv_chans(n)].unsqueeze(2).to_broadcast([P, gs.stop - gs.start, B, BANK_CHANS])
                    pool.wait_ge(conv_added, n + 1 + part)
                    pool.tensor_tensor(hc, hc, pc, ALU.add).then_inc(p_added, 1)
            pool.wait_ge(gates_in, 48)

            def main(i, par):
                if live(i - 1):
                    pool.wait_ge(xg_done, i)
                    for p, bs in pieces(i - 1):
                        pool.wait_ge(s2_done, i + p)
                        pool.tensor_tensor(xr[:, 1 - par, bs, :], s1[:, bs, :], xr[:, 1 - par, bs, :], ALU.add).then_inc(x2_done, 1)
                if latest(i):
                    for p, bs in pieces(i - 1):
                        rsqrt(1, i + p, 1 - par, bs)
                if live(i - 2):
                    for p, bs in pieces(i - 2):
                        pool.wait_ge(tanh_done, i - 1 + p)
                        pool.tensor_tensor(tb_of(i - 2)[:, bs, :], tb_of(i - 2)[:, bs, :], gb_t[:, bs, :], ALU.mult).then_inc(gated, 1)
                if live(i - 1) and not latest(i):
                    rsqrt(1, i, 1 - par)
                if live(i + 1):
                    rsqrt(0, i + 2, 1 - par)
                if live(i):
                    if isinstance(i, int):
                        pool.wait_ge(xr_in[par], (i // 2 + 1) * 16)
                    elif par == 0:
                        pool.wait_ge(xr_in[0], i * 8 + 16)
                    else:
                        pool.wait_ge(xr_in[1], i * 8 + 8)
                    pool.tensor_tensor(xr[:, par, :, :], xr[:, par, :, :], gab2_t[:, :, :], ALU.add).then_inc(xg_done, 1)

            sweep(pool, main, **STEPS)

        @block.scalar
        def _(act):
            with nc.allow_non_contiguous_dma(reason="columns of a few hundred words, once"):
                for k in range(KB):
                    act.dma_start(condT[:, k, :], cond[:, k * P:(k + 1) * P].rearrange("b p -> p b")).then_inc(cond_in, 16)
                act.dma_start(logs[top, 0:1], log_tau.unsqueeze(1)).then_inc(logs_in, 16)
                act.dma_start(logs[bot, 0:1], log_tau.unsqueeze(1)).then_inc(logs_in, 16)
                act.dma_start(logs[:, 1:2], bass.AP(tensor=log_dt.tensor, offset=0, ap=[[0, P], [1, 1]])).then_inc(logs_in, 16)

            act.wait_ge(cond_in, 16 * KB)
            act.activation(sil[:, 0, :, :], condT[:, :, :], ACT.Exp, scale=-1.0).then_inc(cond_exp, 1)
            act.wait_ge(sp_step, 1)
            act.activation(spl[:, 1, :], spl[:, 0, :], ACT.Exp, scale=-1.0).then_inc(log_exp, 1)
            act.wait_ge(sp_step, N_SP)
            act.wait_ge(tables_set, POOL_TABLES)
            act.activation(decay[:, 0, :], times[:, 0, :], ACT.Exp, scale=nega[:, 0:1])
            act.activation(decay[top, 1, :], times[top, 1, :], ACT.Exp, scale=nega[top, 0:1])
            act.activation(decay[bot, 1, 0:HALF], times[bot, 1, 0:HALF], ACT.Exp, scale=nega[bot, 0:1])
            act.activation(decay[:, 2, 0:G], times[:, 3, 0:G], ACT.Exp, scale=nega[:, 0:1])
            act.activation(e_y[top, :], times[top, 2, :], ACT.Exp, scale=nega[top, 0:1])
            act.activation(e_y[bot, HALF:P], times[bot, 2, HALF:P], ACT.Exp, scale=nega[bot, 0:1]).then_inc(decay_done, 1)

            def normed(out_of, in_of, which, par, done, bs=slice(0, B)):
                for b in range(bs.start, bs.stop):
                    last = act.activation(out_of[:, b, :], in_of[:, b, :], ACT.Identity,
                                          bias=nmr[:, par, which, b:b + 1], scale=rstd[:, par, which, b:b + 1])
                last.then_inc(done, 1)

            def z_of(k, par):
                act.wait_ge(nmr_both, k + 1)
                if after(k - 2):
                    act.wait_ge(h_done, k - 1)
                normed(z[:, par, :, :], group(h, k), 0, par, z_done)

            def half_states_of(k, par):
                act.wait_ge(z_mm, k + 1)
                if after(k - 2):
                    act.wait_ge(y_mul, k - 1)
                act.copy(st[bot, par, :, :], z_bank(par)[bot, :, :]).then_inc(st_done, 1)

            def zh_of(k, par):
                act.wait_ge(nmr_both, k + 3)
                normed(group(zh, k), group(h, k), 1, par, zh_done)

            def step(t, par):
                if live(t - 2):
                    half_states_of(t - 2, par)
                if live(t + 2):
                    z_of(t + 2, par)
                if live(t):
                    zh_of(t, par)

            def times_table(r):
                act.wait_ge(p_mm, r + 1)
                act.copy(p_tab[:, r * B:(r + 1) * B, :], by_batch((fo, f1)[r % 2])).then_inc(p_done, 1)

            step(-2, 0)
            act.wait_ge(ffn_tr, 1)
            act.copy(wT[:, :, :, :].rearrange("p a k c -> p a (k c)"), fo).then_inc(ffn_trd, 1)
            step(-1, 1)
            act.wait_ge(sums_done, 1)
            act.wait_ge(tables_set, POOL_TABLES)
            for g in range(G):
                last = act.activation(f_all[top, g, :], f_first[:, :], ACT.Identity,
                                      bias=gk[:, 1, g:g + 1], scale=decay[top, 2, g:g + 1])
            last.then_inc(f_ready, 1)
            act.wait_ge(ffn_mm, 1)
            act.copy(m12[:, :, :].rearrange("p k c -> p (k c)"), f1[:, 0, :]).then_inc(m12_done, 1)
            act.wait_ge(mod_mm, 2)
            step(0, 0)
            act.wait_ge(ffn_mm, 2)
            act.copy(wf[:, :, :].rearrange("p k c -> p (k c)"), f1[:, 1, :]).then_inc(wf_done, 1)
            times_table(0)
            times_table(1)
            step(1, 1)
            for r in range(2, G // B):
                times_table(r)
            assert KB * NMOD * C >= 2 * B * C
            act.wait_ge(k_ready, 1)
            act.wait_ge(mod_out, 16)
            act.wait_ge(wf_split, 1)
            sweep(act, step, **FIRST_STEPS)

            act.wait_ge(y_added, G)
            for q, dst in enumerate(weight_banks(fc1_hi, fc2_hi)):
                act.wait_ge(wt_tr, q + 1)
                act.copy(dst, tr[:, q % 2, :]).then_inc(wt_hi, 1)

            act.wait_ge(conv_added, CONV_BANKS)

            def main(i, par):
                def gelu(m):
                    act.wait_ge(fc1_mm, i * MB + m + 1)
                    if m >= 2 or after(i - 1):
                        act.wait_ge(hid_split, i * MB + m - 1)
                    act.activation(gel[:, m % 2, :], f1[:, m % 2, :], ACT.Gelu, bias=fc1b_c[:, m:m + 1]).then_inc(gelu_done, 1)

                def channel_modulated(k, bs=slice(0, B)):
                    for b in range(bs.start, bs.stop):
                        last = act.activation(fT[:, k, b * P:(b + 1) * P], zfT_block(i - 1, k, b), ACT.Identity,
                                              bias=sb_c[:, k, b:b + 1], scale=cb_c[:, k, b:b + 1])
                    last.then_inc(fT_done, 1)

                def tanh():
                    for p, bs in pieces(i - 2):
                        act.wait_ge(fb_done, i - 1 + p)
                        act.activation(tb_of(i - 2)[:, bs, :], tb_of(i - 2)[:, bs, :], ACT.Tanh).then_inc(tanh_done, 1)

                if live(i):
                    gelu(0)
                if live(i - 2) and not latest(i):
                    tanh()
                if live(i):
                    for m in range(1, 4):
                        gelu(m)
                if live(i - 1):
                    for p, bs in pieces(i - 1):
                        act.wait_ge(nmr_done[1], i + p)
                        normed(zf, xr[:, 1 - par, :, :], 1, 1 - par, zf_done, bs)
                if live(i):
                    gelu(4)
                    gelu(5)
                if live(i + 1):
                    act.wait_ge(nmr_done[0], i + 2)
                    normed(zn, group(h, i + 1), 0, 1 - par, zn_done)
                if live(i):
                    gelu(6)
                if live(i - 1):
                    act.wait_ge(zf_tr, i)
                    if isinstance(i, int) and i == 1:
                        act.wait_ge(mod_columns_in, 16 * 2 * KB)
                if live(i):
                    if live(i - 1):
                        channel_modulated(0)
                    gelu(7)
                    if live(i - 1):
                        channel_modulated(1)
                elif live(i - 1):
                    for p, bs in pieces(i - 1):
                        act.wait_ge(zf_tr, i + p)
                        channel_modulated(0, bs)
                        channel_modulated(1, bs)
                    tanh()
                if live(i + 1):
                    act.wait_ge(zn_tr, i + 2)
                    if isinstance(i, int) and i == -1:
                        act.wait_ge(columns_in, 64)
                    for k in range(KB):
                        last = act.activation(gT[:, k, :], tr[:, k, :], ACT.Identity,
                                              bias=n2b_c[:, k:k + 1], scale=n2w_c[:, k:k + 1])
                    last.then_inc(gT_done, 1)

            sweep(act, main, **STEPS)

        @block.vector
        def _(v):
            def aggregate(which, bn_sem, parts_sem, mv_sem, ve_sem, n, bs=slice(0, B)):
                _, m0, s0, _, m1, s1_ = (bn[:, which, bs, i] for i in range(6))
                both, apart, spread_ = (mv[:, i, which, bs] for i in range(3))
                v.wait_ge(bn_sem, n)
                v.tensor_tensor(both, m0, m1, ALU.add)
                v.tensor_tensor(apart, m0, m1, ALU.subtract)
                v.scalar_tensor_tensor(spread_, s0, C * EPS, s1_, ALU.add, ALU.add).then_inc(parts_sem, 1)
                v.wait_ge(parts_sem, n)
                v.scalar_tensor_tensor(apart, apart, 0.25, apart, ALU.mult, ALU.mult).then_inc(mv_sem, 1)
                v.wait_ge(mv_sem, n)
                v.scalar_tensor_tensor(ve[:, which, bs], spread_, 1.0 / C, apart, ALU.mult, ALU.add).then_inc(ve_sem, 1)

            def bn_of(src, which, bs=slice(0, B)):
                for b in range(bs.start, bs.stop):
                    last = v.bn_stats(bn[:, which, b, :], src[:, b, :])
                return last

            def statistics_of(t, par):
                if live(t + 2):
                    if isinstance(t, int):
                        v.wait_ge(x_in[par], 16 * ((t + 2) // 2 + 1))
                    elif par == 0:
                        v.wait_ge(x_in[0], t * 8 + 32)
                    else:
                        v.wait_ge(x_in[1], t * 8 + 24)
                    last = bn_of(group(h, t + 2), 0)
                if live(t):
                    v.wait_ge(h_done, t + 1)
                    last = bn_of(group(h, t), 1)
                if live(t + 2) or live(t):
                    last.then_inc(bn_both, 1)
                    aggregate(kinds(t), bn_both, parts_both, mv_both, ve_both, t + 3)

            def rest_of(t, par):
                if live(t - 2):
                    if isinstance(t, int) and t == 2:
                        v.wait_ge(dg_done, 1)
                    v.wait_ge(z_mm, t - 1)
                    if after(t - 3):
                        v.wait_ge(carried, t - 2)
                        v.wait_ge(y_mul, t - 2)
                    v.scalar_tensor_tensor(st[top, 1 - par, :, :], st[top, par, :, :], d_g[:, 0:1], z_bank(par)[top, :, :],
                                           ALU.mult, ALU.add).then_inc(carried, 1)
                if live(t - 3):
                    v.wait_ge(y_mm, t - 2)
                    v.tensor_tensor(group(h, t - 3), group(h, t - 3), by_batch(f1), ALU.add).then_inc(y_added, 1)
                if live(t + 2) or live(t):
                    v.wait_ge(rstd_both, t + 3)
                    v.scalar_tensor_tensor(nmr[:, par, kinds(t), :], mv[:, 0, kinds(t), :], -0.5, rstd[:, par, kinds(t), :],
                                           ALU.mult, ALU.mult).then_inc(nmr_both, 1)
                if live(t - 2):
                    v.wait_ge(st_done, t - 1)
                    if after(t - 4):
                        v.wait_ge(y_mm, t - 3)
                    v.tensor_tensor(ym[:, par, :, :], st[:, par, :, :], over_batches(mixw[:, :]), ALU.mult) \
                        .then_inc(y_mul, 1)

            def step(t, par):
                statistics_of(t, par)
                rest_of(t, par)

            v.wait_ge(cond_exp, 1)
            v.tensor_scalar(sil[:, 0, :, :], sil[:, 0, :, :], 1.0, None, ALU.add).then_inc(sil_step, 1)
            v.wait_ge(sil_step, 1)
            v.reciprocal(sil[:, 1, :, :], sil[:, 0, :, :]).then_inc(sil_step, 1)
            v.wait_ge(sil_step, 2)
            v.tensor_tensor(sil[:, 0, :, :], sil[:, 1, :, :], condT[:, :, :], ALU.mult).then_inc(sil_step, 1)

            statistics_of(-2, 0)

            done = [0]

            def chain(ins):
                done[0] += 1
                ins.then_inc(sp_step, 1)
                v.wait_ge(sp_step, done[0])

            absx, y, den, s, s2, q, pos = (spl[:, i, :] for i in range(7))
            v.wait_ge(logs_in, 48)
            chain(v.scalar_tensor_tensor(absx, logs[:, :], -1.0, logs[:, :], ALU.mult, ALU.max))
            v.wait_ge(log_exp, 1)
            chain(v.tensor_scalar(den, y, 2.0, None, ALU.add))
            chain(v.reciprocal(s2, den))
            chain(v.tensor_tensor(s, y, s2, ALU.mult))
            chain(v.tensor_tensor(s2, s, s, ALU.mult))
            chain(v.tensor_scalar(q, s2, 1.0 / (2 * LOG1P_TERMS + 1), None, ALU.mult))
            steps = [0]

            def mod(ins):
                steps[0] += 1
                ins.then_inc(mod_step, 1)
                v.wait_ge(mod_step, steps[0])

            def mod_bank(i, r):
                return v.tensor_copy(modr[:, 2 * i:2 * i + 2, :].rearrange("b a c -> b (a c)"), r)

            v.wait_ge(mod_mm, 1)
            mod(mod_bank(0, acc[0:B, 0, :]))
            v.tensor_scalar(modr[:, CA, :], modr[:, CA, :], 1.0, None, ALU.add).then_inc(mod_a_rows, 1)

            for j in range(LOG1P_TERMS - 1, 0, -1):
                chain(v.scalar_tensor_tensor(q, q, 1.0 / (2 * j + 1), s2, ALU.add, ALU.mult))
            chain(v.scalar_tensor_tensor(q, q, 1.0, s, ALU.add, ALU.mult))
            chain(v.tensor_scalar(pos, logs[:, :], 0.0, None, ALU.max))
            chain(v.scalar_tensor_tensor(q, q, 2.0, pos, ALU.mult, ALU.add))
            chain(v.scalar_tensor_tensor(nega[:, 0:1], q[:, 0:1], -1.0, q[:, 1:2], ALU.mult, ALU.mult))

            rest_of(-2, 0)
            statistics_of(-1, 1)
            v.wait_ge(mod_mm, 2)
            mod_bank(1, acc[0:B, 1, :])
            mod_bank(2, f1[0:B, 0, :]).then_inc(mod_copied, 1)

            def gate_rows():
                v.wait_ge(mod_copied, 1)
                v.tensor_scalar(modr[:, CB, :], modr[:, CB, :], 1.0, None, ALU.add)
                gates = modr[:, GA:GB + 1:GB - GA, :]
                sign, size = gtmp[:, 0, :, :], gtmp[:, 1, :, :]
                v.tensor_scalar(sign, gates, 0.0, 2.0, ALU.is_ge, ALU.mult)
                mod(v.scalar_tensor_tensor(size, gates, -1.0, gates, ALU.mult, ALU.max))
                mod(v.tensor_scalar(size, size, GATE_MIN, None, ALU.max))
                mod(v.scalar_tensor_tensor(gates, sign, -1.0, size, ALU.add, ALU.mult))
                v.wait_ge(b2_in, 16)
                v.tensor_tensor(modr[:, GAB2, :], modr[:, GA, :], b2r[:, :], ALU.mult).then_inc(mod_rows, 1)

            v.wait_ge(decay_done, 1)
            v.tensor_tensor_scan(f_first[:, :], ones[top, :], decay[top, 0, :], 0.0, ALU.mult, ALU.add).then_inc(f_step, 1)
            v.wait_ge(f_step, 1)
            v.tensor_scalar(gk[:, 0, 0:G], decay[top, 2, 0:G], f_first[:, P - 1:P], None, ALU.mult).then_inc(f_step, 1)
            v.wait_ge(f_step, 2)
            v.tensor_tensor_scan(gk[:, 1, 1:G + 1], ones[top, 0:G], gk[:, 0, 0:G], 0.0, ALU.mult, ALU.add).then_inc(sums_done, 1)

            rest_of(-1, 1)
            v.wait_ge(mix_tr, 1)
            v.wait_ge(norm1_in, 80)
            mixps = f1[:, 1, 0:C]
            v.tensor_tensor(mixw[:, :], mixps, n1w_t[:, :], ALU.mult)
            v.tensor_tensor(mixb[top, :], mixps[top, :], n1b_t[top, :], ALU.mult)
            v.tensor_tensor(mixb[HALF:HALF + 1, :], drow[HALF:HALF + 1, :], n1b_t[HALF:HALF + 1, :], ALU.mult).then_inc(mix_step, 1)
            v.wait_ge(wz_tr, 1)
            v.tensor_copy(w_z[:, :], tr[:, 0, 0:P]).then_inc(wz_done, 1)
            v.tensor_copy(d_g[:, :], decay[top, 2, 1:2]).then_inc(dg_done, 1)
            v.tensor_tensor(dcol[:, 0, :], dcol[:, 0, :], dcol[:, 1, :], ALU.mult).then_inc(k_step, 1)
            v.wait_ge(k_mm, 1)
            v.tensor_copy(kpad[:, :, HALF - 1:P - 1], tr[:, 1, 0:P].rearrange("p (k d) -> p k d", k=KB)).then_inc(k_step, 1)
            v.wait_ge(k_step, 2)
            v.tensor_tensor(kpad[:, :, HALF - 1], kpad[:, :, HALF - 1], dcol[:, 0, :], ALU.add).then_inc(k_ready, 1)
            step(0, 0)
            gate_rows()
            step(1, 1)
            v.wait_ge(wf_done, 1)
            v.tensor_copy(wf_hi[:, :, :], wf[:, :, :]).then_inc(f_step, 1)
            v.wait_ge(f_step, 3)
            v.tensor_tensor(wf_lo[:, :, :], wf[:, :, :], wf_hi[:, :, :].bitcast(F32), ALU.subtract).then_inc(wf_split, 1)

            sweep(v, step, **FIRST_STEPS)

            def statistics(src, which, n, bs=slice(0, B)):
                bn_of(src, which, bs).then_inc(bn_done[which], 1)
                aggregate(which, bn_done[which], parts_done[which], mv_done[which], ve_done[which], n, bs)

            def shift(which, n, par, bs=slice(0, B)):
                v.wait_ge(rstd_done[which], n)
                v.scalar_tensor_tensor(nmr[:, par, which, bs], mv[:, 0, which, bs], -0.5, rstd[:, par, which, bs],
                                       ALU.mult, ALU.mult).then_inc(nmr_done[which], 1)

            def low_part(lo, whole, hi, done):
                v.tensor_tensor(lo, whole, hi.bitcast(F32), ALU.subtract).then_inc(done, 1)

            lows = weight_banks(fc1_lo, fc2_lo)
            highs = weight_banks(fc1_hi, fc2_hi)
            v.wait_ge(y_added, G)
            for n in range(CONV_BANKS):
                v.wait_ge(conv_mm, n + 1)
                for gs in by_parts(n):
                    hc = h[:, gs, :, conv_chans(n)].rearrange("p g b c -> p (g b) c")
                    bank = conv_bank(n).rearrange("p (c t) -> p t c", t=TILES)[:, gs.start * B:gs.stop * B, :]
                    v.tensor_tensor(hc, hc, bank, ALU.add).then_inc(conv_added, 1)
                q = weight_bank_at(n)
                if q is not None:
                    v.wait_ge(wt_hi, q + 1)
                    low_part(lows[q], tr[:, q % 2, :], highs[q], wt_lo)

            def main(i, par):
                def split_hidden(m):
                    ring = m % HID_RING
                    v.wait_ge(gelu_done, i * MB + m + 1)
                    if m >= HID_RING or after(i - 1):
                        v.wait_ge(fc2_mm, i * MB + m + 1 - HID_RING)
                    v.tensor_copy(hid_hi[:, ring, :], gel[:, m % 2, :]).then_inc(hid_hi_done, 1)
                    v.wait_ge(hid_hi_done, i * MB + m + 1)
                    low_part(hid_lo[:, ring, :], gel[:, m % 2, :], hid_hi[:, ring, :], hid_split)

                def biased():
                    if after(i - 3) and tb_of(i - 2) is tb:
                        v.wait_ge(stored, 16 * (i - 2))
                    for p, bs in pieces(i - 2):
                        v.wait_ge(f_mm, i - 1 + p)
                        v.tensor_tensor(tb_of(i - 2)[:, bs, :], by_batch(fo)[:, bs, :], over_batches(fb_t[:, :])[:, bs, :], ALU.add) \
                            .then_inc(fb_done, 1)

                def output():
                    for p, bs in pieces(i - 2):
                        v.wait_ge(gated, i - 1 + p)
                        v.tensor_tensor(tb_of(i - 2)[:, bs, :], tb_of(i - 2)[:, bs, :], xr[:, par, bs, :], ALU.add) \
                            .then_inc(out_done, 1)

                if live(i - 1):
                    v.wait_ge(fc2_mm, i * MB)
                    if after(i - 2):
                        v.wait_ge(x2_done, i - 1)
                    for p, bs in pieces(i - 1):
                        v.tensor_tensor(s1[:, bs, :], by_batch(acc)[:, bs, :], group(h, i - 1)[:, bs, :], ALU.add).then_inc(s1_done, 1)
                        v.wait_ge(s1_done, i + p)
                        v.tensor_tensor(s1[:, bs, :], s1[:, bs, :], ga_t[:, bs, :], ALU.mult).then_inc(s2_done, 1)
                if live(i - 2) and not latest(i):
                    biased()
                if live(i):
                    split_hidden(0)
                if live(i - 1):
                    for p, bs in pieces(i - 1):
                        v.wait_ge(x2_done, i + p)
                        statistics(xr[:, 1 - par, :, :], 1, i + p, bs)
                if live(i):
                    split_hidden(1)
                if latest(i):
                    for p, bs in pieces(i - 1):
                        shift(1, i + p, 1 - par, bs)
                    biased()
                if live(i - 2) and not latest(i):
                    output()
                if live(i - 1) and not latest(i):
                    shift(1, i, 1 - par)
                if live(i):
                    split_hidden(2)
                if live(i + 1):
                    if isinstance(i, int) and i == 0:
                        v.wait_ge(p_added, CONV_BANKS + 1)
                    statistics(group(h, i + 1), 0, i + 2)
                if live(i):
                    split_hidden(3)
                if live(i + 1):
                    shift(0, i + 2, 1 - par)
                if live(i):
                    for m in range(4, 8):
                        split_hidden(m)
                if live(i - 1):
                    for p, bs in pieces(i - 1):
                        v.wait_ge(fT_done, KB * (i + p))
                        tokens = slice(bs.start * P, bs.stop * P)
                        v.tensor_copy(f_hi[:, :, tokens], fT[:, :, tokens]).then_inc(f_hi_done, 1)
                        v.wait_ge(f_hi_done, i + p)
                        low_part(f_lo[:, :, tokens], fT[:, :, tokens], f_hi[:, :, tokens], f_split)
                if latest(i):
                    output()
                if live(i + 1):
                    v.wait_ge(gT_done, i + 2)
                    if after(i):
                        v.wait_ge(fc1_mm, (i + 1) * MB)
                    v.tensor_copy(g_hi[:, :, :], gT[:, :, :]).then_inc(g_hi_done, 1)
                    v.wait_ge(g_hi_done, i + 2)
                    low_part(g_lo[:, :, :], gT[:, :, :], g_hi[:, :, :], g_split)

            v.wait_ge(p_added, CONV_BANKS)
            v.wait_ge(columns_in, 64)
            sweep(v, main, **STEPS)

        @block.tensor
        def _(pe):
            def mm(o, lhs, rhs, start, stop):
                return pe.matmul(o, lhs, rhs, start=start, stop=stop)

            pe.wait_ge(sil_step, 3)
            for i, bank in enumerate((acc[0:B, 0, :], acc[0:B, 1, :], f1[0:B, 0, :])):
                pe.wait_ge(wmod_in if i else wmod_a_in, 16)
                for k in range(KB):
                    last = mm(bank, sil[:, 0, k, :], wm[:, k, i * BANK:(i + 1) * BANK], k == 0, k == KB - 1)
                if i != 1:
                    last.then_inc(mod_mm, 1)
            pe.wait_ge(ident_set, 1)
            pe.wait_ge(mix_in, 32)
            for k in range(KB):
                last = pe.transpose(f1[:, 1, k * P:(k + 1) * P], mixn[:, k, :, :].rearrange("p a n -> p (a n)"), ident[:, :])
            last.then_inc(mix_tr, 1)
            pe.wait_ge(decay_done, 1)
            pe.transpose(tr[:, 0, 0:P], decay[:, 1, :], ident[:, :]).then_inc(wz_tr, 1)
            pe.wait_ge(ffn_in, 48)
            for i in range(2):
                for kc in range(KB):
                    for kd in range(KB):
                        last = pe.transpose(fo[:, i, kd * C + kc * P:kd * C + (kc + 1) * P],
                                            wn[:, i, kc, kd * P:(kd + 1) * P], ident[:, :])
            last.then_inc(ffn_tr, 1)
            pe.wait_ge(mix_step, 1)
            for k in range(KB):
                last = mm(tr[:, 1, k * HALF:(k + 1) * HALF], mixw[top, k * P:(k + 1) * P], decay[top, 0, 0:HALF], True, True)
            last.then_inc(k_mm, 1)
            pe.wait_ge(ffn_trd, 1)
            pe.wait_ge(mod_copied, 1)
            for i, rhs in ((1, wn[:, 2, :, :]), (0, m12[:, :, :])):
                if i == 0:
                    pe.wait_ge(m12_done, 1)
                for r in range(KB):
                    for k in range(KB):
                        last = mm(f1[:, 1 - i, r * C:(r + 1) * C], wT[:, i, k, r * P:(r + 1) * P], rhs[:, k, :], k == 0, k == KB - 1)
                last.then_inc(ffn_mm, 1)

            def times_table(r):
                if r >= 2:
                    pe.wait_ge(p_done, r - 1)
                for b in range(B):
                    last = mm(by_batch((fo, f1)[r % 2])[:, b, :], f_all[0:HALF + 1, r * B + b, :], mixb[0:HALF + 1, :], True, True)
                last.then_inc(p_mm, 1)

            def states_of(k, par):
                pe.wait_ge(zh_done, k + 1)
                if after(k - 2):
                    pe.wait_ge(st_done, k - 1)
                    pe.wait_ge(carried, k - 1)
                for b in range(B):
                    last = mm(z_bank(par)[:, b, :], w_z[:, :], group(zh, k)[:, b, :], True, True)
                last.then_inc(z_mm, 1)

            def y_of(k, par):
                pe.wait_ge(y_mul, k + 1)
                if after(k - 1):
                    pe.wait_ge(y_added, k)
                else:
                    pe.wait_ge(p_done, G // B)
                for b in range(B):
                    last = mm(by_batch(f1)[:, b, :], e_y[:, :], ym[:, par, b, :], True, True)
                last.then_inc(y_mm, 1)

            def step(t, par):
                if live(t - 2):
                    y_of(t - 2, par)
                if live(t):
                    states_of(t, par)

            pe.wait_ge(f_ready, 1)
            for r in range(G // B):
                if r == 1:
                    pe.wait_ge(wf_done, 1)
                if r == 2:
                    pe.wait_ge(k_ready, 1)
                    step(0, 0)
                times_table(r)
            step(1, 1)
            sweep(pe, step, **dict(FIRST_STEPS, last=G))

            def transpose_weights(q):
                pe.wait_ge(fc_in[q % 2], 16 * (q // 2 + 1))
                if q >= 2:
                    pe.wait_ge(wt_lo, q - 1)
                for j in range(4):
                    to = j if q < FC1_BANKS else j % 2 * 2 + j // 2
                    last = pe.transpose(tr[:, q % 2, to * P:(to + 1) * P], w_raw[:, q % 2, j * P:(j + 1) * P], ident[:, :])
                last.then_inc(wt_tr, 1)

            def convolve(n):
                if n >= len(CONV_RING):
                    pe.wait_ge(conv_added, n + 1 - len(CONV_RING))
                for c in range(n * BANK_CHANS, (n + 1) * BANK_CHANS):
                    ring, place = c // SLOT_CHANS % SLOTS, c % SLOT_CHANS
                    if place == 0:
                        pe.wait_ge(toep_in[ring], 32 * (c // SLOT_CHANS // SLOTS + 1))
                    col = c % BANK_CHANS * TILES
                    for half in (top, bot):
                        last = mm(conv_bank(n)[half, col:col + TILES], toep[half, ring, place, :],
                                  zh[half, :, :, c].rearrange("p g b -> p (g b)"), True, True)
                last.then_inc(conv_mm, 1)

            convolve(0)
            convolve(1)
            y_of(G - 1, (G - 1) % 2)
            for n in range(2, CONV_BANKS):
                if n == 4:
                    pe.wait_ge(y_added, G)
                convolve(n)
                if weight_bank_at(n) is not None:
                    transpose_weights(weight_bank_at(n))

            def transposes(dst, src, ready, n, done, bs=slice(0, B)):
                pe.wait_ge(ready, n)
                for k in range(KB):
                    for b in range(bs.start, bs.stop):
                        last = pe.transpose(dst(k, b), src[:, b, k * P:(k + 1) * P], ident[:, :])
                last.then_inc(done, 1)

            def main(i, par):
                def fc1(m):
                    if m == 0:
                        pe.wait_ge(g_split, i + 1)
                    if m >= 2 or after(i - 1):
                        pe.wait_ge(gelu_done, i * MB + m - 1)
                    terms = [(w, g, k) for k in range(KB) for w, g in ((fc1_hi, g_hi), (fc1_hi, g_lo), (fc1_lo, g_hi))]
                    for n, (w, g, k) in enumerate(terms):
                        last = mm(f1[:, m % 2, :], w[:, k, m * P:(m + 1) * P], g[:, k, :], n == 0, n == len(terms) - 1)
                    last.then_inc(fc1_mm, 1)

                def fc2(m):
                    ring = m % HID_RING
                    pe.wait_ge(hid_split, i * MB + m + 1)
                    if m == 0 and after(i - 1):
                        pe.wait_ge(s1_done, i)
                    for b in range(B):
                        for n, (w, g) in enumerate(((fc2_hi, hid_hi), (fc2_lo, hid_hi), (fc2_hi, hid_lo))):
                            last = pe.matmul(by_batch(acc)[:, b, :], g[:, ring, b * P:(b + 1) * P], w[:, m, :],
                                             start=m == 0 and n == 0 and b % 2 == 0, stop=m == MB - 1 and n == 2,
                                             skip_group_check=True)
                    last.then_inc(fc2_mm, 1)

                if live(i):
                    for m in range(6):
                        fc1(m)
                        if m >= FC2_LAG:
                            fc2(m - FC2_LAG)
                if live(i - 1):
                    if after(i - 2) and not latest(i):
                        pe.wait_ge(fb_done, i - 1)
                    for p, bs in pieces(i - 1):
                        transposes(lambda k, b: zfT_block(i - 1, k, b), zf, zf_done, i + p, zf_tr, bs)
                if live(i):
                    for m in range(6, MB):
                        fc1(m)
                        fc2(m - FC2_LAG)
                if live(i + 1):
                    if after(i):
                        pe.wait_ge(gT_done, i + 1)
                    transposes(lambda k, b: tr[:, k, b * P:(b + 1) * P], zn, zn_done, i + 2, zn_tr)
                if live(i):
                    for m in range(MB - FC2_LAG, MB):
                        fc2(m)
                if live(i - 1):
                    if latest(i):
                        pe.wait_ge(fb_done, i - 1)
                    for p, bs in pieces(i - 1):
                        pe.wait_ge(f_split, i + p)
                        for b in range(bs.start, bs.stop):
                            terms = [(g, w, k) for k in range(KB) for g, w in ((f_hi, wf_hi), (f_hi, wf_lo), (f_lo, wf_hi))]
                            for n, (g, w, k) in enumerate(terms):
                                last = mm(by_batch(fo)[:, b, :], g[:, k, b * P:(b + 1) * P], w[:, k, :], n == 0, n == len(terms) - 1)
                        last.then_inc(f_mm, 1)

            pe.wait_ge(conv_added, CONV_BANKS)
            pe.wait_ge(wt_lo, WEIGHT_BANKS)
            sweep(pe, main, **STEPS)


_INS = ["L0_attn_x", "L0_attn_log_tau", "L0_attn_log_dt", "L0_attn_mix", "L0_attn_D", "L0_attn_norm1_w", "L0_attn_norm1_b",
        "L0_attn_norm2_w", "L0_attn_norm2_b", "L0_attn_fc1_w", "L0_attn_fc1_b", "L0_attn_fc2_w", "L0_attn_fc2_b",
        "L0_ffn_weight", "L0_ffn_aux_weight1", "L0_ffn_aux_weight2", "L0_ffn_bias", "L0_c", "L0_wmod"]


def kernel(**inputs):
    import numpy as _np
    import concourse.bacc as _bacc
    from concourse import mybir as _mybir
    from concourse.bass_utils import run_bass_kernel_spmd as _run

    nc = _bacc.Bacc("TRN2", target_bir_lowering=False, num_devices=1)
    arrays, args = {}, []
    for name in _INS:
        a = _np.ascontiguousarray(inputs[name])
        if a.ndim == 0:
            a = a.reshape(1)
        arrays[f"in_{name}_dram"] = a
        args.append(nc.dram_tensor(f"in_{name}_dram", a.shape, _mybir.dt.from_np(a.dtype), kind="ExternalInput").ap())
    shape = inputs["L0_attn_x"].shape
    args.append(nc.dram_tensor("out_0_dram", shape, _mybir.dt.float32, kind="ExternalOutput").ap())
    adaln_block(nc, *args)
    r = _run(nc, [arrays], core_ids=[0])
    return r.results[0]["out_0_dram"]
```
